# Optimizing a Trainium2 kernel written in Bass

```python
import numpy as np
import jax
import jax.numpy as jnp

def _softmax(x, axis=-1):
    return jax.nn.softmax(x, axis=axis)

def _gelu(x):
    return jax.nn.gelu(x, approximate=True)

def _silu(x):
    return jax.nn.silu(x)

def _sigmoid(x):
    return jax.nn.sigmoid(x)

def _layernorm(x, axis=-1, eps=1e-05):
    m = jnp.mean(x, axis=axis, keepdims=True)
    v = jnp.var(x, axis=axis, keepdims=True)
    return (x - m) / jnp.sqrt(v + eps)

def _scatter_add(tgt, idx, src, axis=0):
    return tgt.at[idx].add(src)

def _segment_sum(src, seg, n):
    return jax.ops.segment_sum(src, seg, n)
kernel_name = 'mk_cond_resid_d2_seqx_r2_dbef81'

def setup_inputs(seed: int=0):
    np.random.seed(seed)
    _w = jnp.asarray

    def _rec_inputs():
        import jax
        import jax.numpy as jnp
        _rk = jax.random.key(seed)
        x = 7.22e-05 + 1 * jax.random.normal(jax.random.fold_in(_rk, 1), (8, 512, 1024), jnp.float32)
        _lenS = 512 - jax.random.randint(jax.random.fold_in(_rk, 7), (8,), 0, max(1, 512 // 4) + 1, jnp.int32)
        _lenS2 = 512 - jax.random.randint(jax.random.fold_in(_rk, 8), (8,), 0, max(1, 512 // 4) + 1, jnp.int32)
        cond_2048 = jax.random.bernoulli(jax.random.fold_in(_rk, 11), 0.8975, (8, 1024)).astype(jnp.float32)
        return (x, cond_2048)
    x, cond_2048 = _rec_inputs()

    def _L0_cond_setup():
        import math
        import jax, jax.numpy as jnp
        import numpy as np
        ENCODER_SIZE = 512
        NUM_HEADER = 16
        DK = ENCODER_SIZE // NUM_HEADER
        B, S = (4, 1024)
        key = jax.random.key(seed)
        kx, km, kq, kk, kv, ko = jax.random.split(key, 6)
        x = jax.random.normal(kx, (B, ENCODER_SIZE, S), dtype=jnp.float32)
        mask = (jax.random.uniform(km, (B, S)) < 0.9).astype(jnp.float32)
        lim = math.sqrt(6.0 / (ENCODER_SIZE + DK))
        Wq = jax.random.uniform(kq, (NUM_HEADER, ENCODER_SIZE, DK), minval=-lim, maxval=lim, dtype=jnp.float32)
        Wk = jax.random.uniform(kk, (NUM_HEADER, ENCODER_SIZE, DK), minval=-lim, maxval=lim, dtype=jnp.float32)
        Wv = jax.random.uniform(kv, (NUM_HEADER, ENCODER_SIZE, DK), minval=-lim, maxval=lim, dtype=jnp.float32)
        limo = math.sqrt(6.0 / ENCODER_SIZE)
        Wo = jax.random.uniform(ko, (ENCODER_SIZE, ENCODER_SIZE), minval=-limo, maxval=limo, dtype=jnp.float32)
        return {'x': x, 'mask': mask, 'Wq': Wq, 'Wk': Wk, 'Wv': Wv, 'Wo': Wo}
    _L0_cond_all = _L0_cond_setup()
    _L0_cond_in = {k: v for k, v in _L0_cond_all.items() if k in ('Wq', 'Wk', 'Wv', 'Wo')}
    del _L0_cond_all

    def _L1_cond_setup():
        import jax, jax.numpy as jnp
        import numpy as np
        DT = 0.01
        EPSILON = 0.08
        ALPHA = 0.7
        BETA = 0.8
        CLAMP = 20.0
        B, T, N = (128, 128, 1024)

        def _derivative(q, p, drive, coupling, bias):
            i_couple = jnp.tanh(q) @ coupling.T
            dq = q - q ** 3 / 3.0 - p + drive + i_couple + bias
            dp = EPSILON * (q + ALPHA - BETA * p)
            return (dq, dp)

        def _rk4_step(q, p, drive, coupling, bias):
            dq1, dp1 = _derivative(q, p, drive, coupling, bias)
            dq2, dp2 = _derivative(q + 0.5 * DT * dq1, p + 0.5 * DT * dp1, drive, coupling, bias)
            dq3, dp3 = _derivative(q + 0.5 * DT * dq2, p + 0.5 * DT * dp2, drive, coupling, bias)
            dq4, dp4 = _derivative(q + DT * dq3, p + DT * dp3, drive, coupling, bias)
            q_next = q + DT / 6.0 * (dq1 + 2 * dq2 + 2 * dq3 + dq4)
            p_next = p + DT / 6.0 * (dp1 + 2 * dp2 + 2 * dp3 + dp4)
            q_next = jnp.clip(q_next, -CLAMP, CLAMP)
            p_next = jnp.clip(p_next, -CLAMP, CLAMP)
            return (q_next, p_next)
        key = jax.random.key(seed)
        k1, k2, k3, k4 = jax.random.split(key, 4)
        return {'q0': jax.random.normal(k1, (B, N), dtype=jnp.float32), 'p0': jax.random.normal(k2, (B, N), dtype=jnp.float32), 'input_drive_seq': jax.random.normal(k3, (B, T, N), dtype=jnp.float32), 'coupling': jax.random.normal(k4, (N, N), dtype=jnp.float32) * 0.01, 'bias': jnp.zeros((N,), dtype=jnp.float32)}
    _L1_cond_all = _L1_cond_setup()
    _L1_cond_in = {k: v for k, v in _L1_cond_all.items() if k in ('coupling', 'bias')}
    del _L1_cond_all
    return {'x': x, 'cond_2048': cond_2048, 'L0_cond_Wq': _L0_cond_in['Wq'], 'L0_cond_Wk': _L0_cond_in['Wk'], 'L0_cond_Wv': _L0_cond_in['Wv'], 'L0_cond_Wo': _L0_cond_in['Wo'], 'L1_cond_coupling': _L1_cond_in['coupling'], 'L1_cond_bias': _L1_cond_in['bias']}

def reference(x, cond_2048, L0_cond_Wq, L0_cond_Wk, L0_cond_Wv, L0_cond_Wo, L1_cond_coupling, L1_cond_bias):
    import jax
    import jax.numpy as jnp

    def _L0_cond_ref(x, mask, Wq, Wk, Wv, Wo):
        import math
        import jax, jax.numpy as jnp
        import numpy as np
        ENCODER_SIZE = 512
        NUM_HEADER = 16
        DK = ENCODER_SIZE // NUM_HEADER
        B, S = (4, 1024)
        num_header = Wq.shape[0]
        dk = Wq.shape[2]
        sqrt_dk_inv = 1.0 / math.sqrt(dk)
        xt = jnp.transpose(x, (0, 2, 1))
        q = xt @ Wq[1]
        k = xt @ Wk[1]
        v = xt @ Wv[1]
        scores = jnp.einsum('bqd,bkd->bqk', q, k) * sqrt_dk_inv
        hmask = mask[:, None, :]
        vmask = mask[:, :, None]
        scores = scores * hmask + (1.0 - hmask) * -1e+30
        attn = jax.nn.softmax(scores, axis=2) * vmask
        head = attn @ v
        heads = jnp.tile(head, (1, 1, num_header))
        out = heads @ Wo
        return jnp.transpose(out, (0, 2, 1))

    def _L1_cond_ref(q0, p0, input_drive_seq, coupling, bias):
        import jax, jax.numpy as jnp
        import numpy as np
        DT = 0.01
        EPSILON = 0.08
        ALPHA = 0.7
        BETA = 0.8
        CLAMP = 20.0
        B, T, N = (128, 128, 1024)

        def _derivative(q, p, drive, coupling, bias):
            i_couple = jnp.tanh(q) @ coupling.T
            dq = q - q ** 3 / 3.0 - p + drive + i_couple + bias
            dp = EPSILON * (q + ALPHA - BETA * p)
            return (dq, dp)

        def _rk4_step(q, p, drive, coupling, bias):
            dq1, dp1 = _derivative(q, p, drive, coupling, bias)
            dq2, dp2 = _derivative(q + 0.5 * DT * dq1, p + 0.5 * DT * dp1, drive, coupling, bias)
            dq3, dp3 = _derivative(q + 0.5 * DT * dq2, p + 0.5 * DT * dp2, drive, coupling, bias)
            dq4, dp4 = _derivative(q + DT * dq3, p + DT * dp3, drive, coupling, bias)
            q_next = q + DT / 6.0 * (dq1 + 2 * dq2 + 2 * dq3 + dq4)
            p_next = p + DT / 6.0 * (dp1 + 2 * dp2 + 2 * dp3 + dp4)
            q_next = jnp.clip(q_next, -CLAMP, CLAMP)
            p_next = jnp.clip(p_next, -CLAMP, CLAMP)
            return (q_next, p_next)
        drive_tbn = jnp.swapaxes(input_drive_seq, 0, 1)

        def scan_fn(carry, drive):
            q, p = carry
            q, p = _rk4_step(q, p, drive, coupling, bias)
            return ((q, p), q)
        (_, _), q_trace_tbn = jax.lax.scan(scan_fn, (q0, p0), drive_tbn)
        return jnp.swapaxes(q_trace_tbn, 0, 1)
    x = x + _L0_cond_ref(x, cond_2048, L0_cond_Wq, L0_cond_Wk, L0_cond_Wv, L0_cond_Wo)
    x = x + _L1_cond_ref(cond_2048, cond_2048, x, L1_cond_coupling, L1_cond_bias)
    return x

_drawn_inputs = setup_inputs


def setup_inputs(seed=0):
    import zlib

    import numpy as np

    out = dict(_drawn_inputs(seed))
    spreads = {'L1_cond_bias': (0.0, 0.1)}
    factors = {}
    for name, (base, spread) in spreads.items():
        noise = np.random.default_rng([zlib.crc32(name.encode()), seed]).standard_normal(out[name].shape)
        drawn = base * np.exp(spread * noise) if base else spread * noise
        out[name] = jnp.asarray(drawn.astype(out[name].dtype))
    for name, factor in factors.items():
        out[name] = (out[name] * factor).astype(out[name].dtype)
    return out
```

```python
import concourse.bass as bass
from concourse import mybir
from contextlib import ExitStack

F32 = mybir.dt.float32
F16 = mybir.dt.float16
I32 = mybir.dt.int32
ALU = mybir.AluOpType
ACT = mybir.ActivationFunctionType
AX = mybir.AxisListType

P = 128
B = 8
T = 512
N = 1024
NC = N // P
KT = T // P
DK = 32
VROW = 2 * DK
HROW = 3 * DK
COLS = NC * B
BANK = 512
NBANK = 8
HALVES = N // BANK
TILES = BANK // P
MASKED = -1e30

DT, EPS, ALPHA, BETA, CLAMP = 0.01, 0.08, 0.7, 0.8, 20.0
SHIFT = ALPHA / BETA
STAGES = 4
STEP = [DT / 2, DT / 2, DT, DT / 6]

CHUNKS = [(0, 1), (1, 5), (5, 8)]
NCH = len(CHUNKS)
ORDER = [(0, 0), (0, 1), (0, 2), (1, 0), (1, 1), (2, 0), (2, 1), (1, 2), (2, 2)]
PIECES = [(0, 5), (5, 8)]
PARTS = 2
TANH_SCALE = 4096.0
COUP_EXP = 14
STORE_STEPS = 32


def build(nc, x, x_pt, cond, cond_p, wq, wk, wv, wo, coupling_t, bias_p, out_pt):
    ctx = ExitStack()
    with ctx:
        def sb(name, shape, dt=F32):
            return ctx.enter_context(nc.sbuf_tensor(name, shape, dt))

        def sem(name):
            return ctx.enter_context(nc.semaphore(name))

        drive = sb("drive", [P, T + 1, COLS])
        coup = sb("coup", [P, NC, PARTS, N], F16)
        tanh_parts = sb("tanh_parts", [P, 2, NC, PARTS, B], F16)

        xb = sb("xb", [P, KT, N])
        w_qkv = sb("w_qkv", [P, KT, 3 * DK])
        qv = sb("qv", [P, N])
        km = sb("km", [P, N])
        q_aug = qv[0:DK + 1, :]
        v_t = qv[VROW:VROW + DK, :]
        head_t = qv[HROW:HROW + DK, 0:BANK]
        wo_sum = qv[HROW:HROW + DK, BANK:BANK + T]
        k_aug = km[0:DK + 1, :]
        mask_bc = km[VROW:VROW + DK + 1, :]
        v_sb = sb("v_sb", [P, NC, DK])
        probs = sb("probs", [P, 2, N])
        probs_t = sb("probs_t", [P, NC, BANK])
        neg_max = sb("neg_max", [P, NC])
        row_sum = sb("row_sum", [P, NC])
        inv_sum = sb("inv_sum", [P, NC])
        row_scale = sb("row_scale", [P, NC])
        ident = sb("ident", [P, P])
        stack = sb("stack", [P, P // DK, DK])
        stack_sum = sb("stack_sum", [P, DK])
        ones_row = sb("ones_row", [1, P])

        col_max = sb("col_max", [P, NC])
        all_max = sb("all_max", [P, 1])
        top = sb("top", [1, 1])
        power = sb("power", [P, 1])
        inv_power = sb("inv_power", [P, 1])
        coup_scale = sb("coup_scale", [P, 1])

        cond_sb = sb("cond_sb", [P, NC, B])
        bias_sb = sb("bias_sb", [P, NC])
        step_scale = sb("step_scale", [P, STAGES])
        q_st = [sb(f"q_st{s}", [P, COLS]) for s in range(STAGES)]
        q_raw = sb("q_raw", [P, COLS])
        half_sum = sb("half_sum", [P, COLS])
        tanh_sb = sb("tanh_sb", [P, COLS])
        square = sb("square", [P, COLS])
        cubic = sb("cubic", [P, COLS])
        base = sb("base", [P, COLS])
        z = sb("z", [P, COLS])
        z2 = sb("z2", [P, COLS])
        z3 = sb("z3", [P, COLS])
        p_st = sb("p_st", [P, COLS])
        p_mid = sb("p_mid", [P, COLS])
        p_raw = sb("p_raw", [P, COLS])
        bias_b = sb("bias_b", [P, COLS])
        drive_b = sb("drive_b", [P, COLS])
        drive_p = sb("drive_p", [P, COLS])
        g = [sb(f"g{s}", [P, COLS]) for s in range(STAGES)]
        y_mid = sb("y_mid", [P, COLS])
        x_sum = sb("x_sum", [P, COLS])
        x_sum2 = sb("x_sum2", [P, COLS])
        x_third = sb("x_third", [P, COLS])
        g_sum = sb("g_sum", [P, COLS])

        ps = ctx.enter_context(nc.psum_tensor("ps", [P, NBANK, BANK], F32))
        score_ps = [ps[:, 0:2, :].rearrange("p a n -> p (a n)"), ps[:, 2:4, :].rearrange("p a n -> p (a n)")]
        turn_ps = [ps[:, 4, :], ps[:, 5, :]]
        head_ps = ps[:, 6, :]
        out_ps = [ps[:, 7, :], ps[:, 6, :]]
        qkv_ps = score_ps[0]
        small_ps = ps[:, 7, :]

        coup_loaded = sem("coup_loaded")
        consts_loaded = sem("consts_loaded")
        wo_loaded = sem("wo_loaded")
        drive_loaded = sem("drive_loaded")
        x_loaded = sem("x_loaded")
        mask_loaded = sem("mask_loaded")
        stored = sem("stored")

        pool_ready = sem("pool_ready")
        stack_ready = sem("stack_ready")
        wo_summed = sem("wo_summed")
        wo_ready = sem("wo_ready")
        maxes_ready = sem("maxes_ready")
        max_turned = sem("max_turned")
        top_ready = sem("top_ready")
        max_spread = sem("max_spread")
        scale_ready = sem("scale_ready")
        coup_high = sem("coup_high")
        coup_low = sem("coup_low")
        setup = sem("setup")

        qkv_done = sem("qkv_done")
        q_ready = sem("q_ready")
        k_ready = sem("k_ready")
        v_copied = sem("v_copied")
        mask_row_ready = sem("mask_row_ready")
        v_turned = sem("v_turned")
        v_ready = sem("v_ready")
        scores_done = sem("scores_done")
        max_ready = sem("max_ready")
        probs_ready = sem("probs_ready")
        turned = [sem("turned0"), sem("turned1")]
        turned_copied = [sem("turned_copied0"), sem("turned_copied1")]
        head_done = sem("head_done")
        head_ready = sem("head_ready")
        inv_ready = sem("inv_ready")
        row_scale_ready = sem("row_scale_ready")
        out_done = sem("out_done")
        out_added = sem("out_added")

        product_done = [sem(f"product_done{j}") for j in range(NCH)]
        half_ready = [sem(f"half_ready{j}") for j in range(NCH)]
        q_next = [sem(f"q_next{j}") for j in range(NCH)]
        tanh_ready = [sem(f"tanh_ready{j}") for j in range(NCH)]
        high_ready = [sem(f"high_ready{j}") for j in range(NCH)]
        parts_ready = [sem(f"parts_ready{j}") for j in range(NCH)]
        square_ready = [sem(f"square_ready{k}") for k in range(len(PIECES))]
        cubic_ready = [sem(f"cubic_ready{k}") for k in range(len(PIECES))]
        base_ready = [sem(f"base_ready{k}") for k in range(len(PIECES))]
        clipped = [sem(f"clipped{k}") for k in range(len(PIECES))]
        z_ready = [sem(f"z_ready{k}") for k in range(len(PIECES))]
        p_ready = sem("p_ready")
        drive_b_ready = sem("drive_b_ready")
        drive_p_ready = sem("drive_p_ready")
        g_ready = [sem(f"g_ready{s}") for s in range(STAGES)]
        p_mid_ready = [sem(f"p_mid_ready{s}") for s in range(STAGES)]
        z2_ready = sem("z2_ready")
        z3_ready = sem("z3_ready")
        z4_ready = [sem(f"z4_ready{k}") for k in range(len(PIECES))]
        y_ready = sem("y_ready")
        x_sum_ready = [sem(f"x_sum_ready{k}") for k in range(STAGES)]
        x_third_ready = sem("x_third_ready")
        g_sum_ready = [sem(f"g_sum_ready{k}") for k in range(3)]
        p_raw_ready = sem("p_raw_ready")
        traced = sem("traced")

        def cols(t, blocks):
            return t[:, B * blocks[0]:B * blocks[1]]

        def by_block(t, blocks):
            return cols(t, blocks).rearrange("p (c b) -> p c b", b=B)

        def product(stage, j, part):
            w = CHUNKS[j][1] - CHUNKS[j][0]
            return ps[:, NCH * (stage % 2) + j, 0:w * PARTS * B].rearrange(
                "p (c t b) -> p c t b", t=PARTS, b=B)[:, :, part, :]

        def coup_stage(c):
            half = probs_t[:, :, :].rearrange("p a n -> p (a n)")[:, (c - KT) * N:(c - KT + 1) * N]
            return xb[:, c, :] if c < KT else half

        block = ctx.enter_context(nc.Block())

        @block.sync
        def _(sp):
            for c in range(NC):
                sp.dma_start(coup_stage(c), coupling_t[P * c:P * (c + 1), :]).then_inc(coup_loaded, 16)
            sp.dma_start(cond_sb[:, :, :], cond_p).then_inc(consts_loaded, 16)
            sp.dma_start(bias_sb[:, :], bias_p).then_inc(consts_loaded, 16)
            for i, w in enumerate((wq, wk, wv)):
                sp.dma_start(w_qkv[:, :, DK * i:DK * (i + 1)],
                             w.rearrange("(c p) d -> p c d", p=P)).then_inc(consts_loaded, 16)
            sp.wait_ge(coup_high, NC)
            sp.wait_ge(coup_low, NC)
            with sp.Fori(0, B) as b:
                sp.wait_ge(qkv_done, b)
                sp.dma_start(xb[:, :, :], x[bass.ds(b, 1), :, :].rearrange("o (c p) n -> p (o c) n", p=P))\
                  .then_inc(x_loaded, 16)
                sp.wait_ge(k_ready, b)
                sp.wait_ge(mask_row_ready, b)
                sp.dma_start(mask_bc[:, :], cond[bass.ds(b, 1), :].broadcast_to([DK + 1, N]))\
                  .then_inc(mask_loaded, 16)
            with sp.Fori(0, T // STORE_STEPS) as i:
                sp.wait_ge(traced, i * STORE_STEPS + STORE_STEPS)
                sp.dma_start(out_pt[:, bass.ds(i * STORE_STEPS, STORE_STEPS), :],
                             drive[:, bass.ds(i * STORE_STEPS, STORE_STEPS), :]).then_inc(stored, 16)
            sp.wait_ge(stored, 16 * (T // STORE_STEPS))

        @block.gpsimd
        def _(pool):
            nc.gpsimd.memset(ident[:, :], 0.0).then_inc(pool_ready, 1)
            pool.wait_ge(pool_ready, 1)
            nc.gpsimd.memset(stack[:, :, :], 0.0).then_inc(pool_ready, 1)
            pool.wait_ge(pool_ready, 2)
            nc.gpsimd.memset(ones_row[:, :], 1.0).then_inc(pool_ready, 1)
            pool.wait_ge(pool_ready, 3)
            nc.gpsimd.memset(q_aug[DK:DK + 1, :], 1.0).then_inc(pool_ready, 1)
            pool.wait_ge(pool_ready, 4)
            nc.gpsimd.memset(drive[:, T, :], 0.0).then_inc(pool_ready, 1)
            pool.wait_ge(pool_ready, 5)
            nc.gpsimd.affine_select(out=ident[:, :], in_=ident[:, :], compare_op=ALU.not_equal, fill=1.0,
                                    base=0, pattern=[[-1, P]], channel_multiplier=1).then_inc(pool_ready, 1)
            pool.wait_ge(pool_ready, 6)
            nc.gpsimd.affine_select(out=stack[:, :, :], in_=stack[:, :, :], compare_op=ALU.not_equal,
                                    fill=1.0, base=0, pattern=[[-DK, P // DK], [-1, DK]],
                                    channel_multiplier=1).then_inc(pool_ready, 1)

        @block.scalar
        def _(act):
            act.dma_start(probs[:, :, :].rearrange("p a (c n) -> p (a c) n", n=T),
                          wo.rearrange("(c p) n -> p c n", p=P)).then_inc(wo_loaded, 16)
            for i in range(8):
                s = slice(i * T // 8, (i + 1) * T // 8)
                act.dma_start(drive[:, s, :], x_pt[:, s, :]).then_inc(drive_loaded, 16)
            act.wait_ge(scale_ready, 1)
            for c in range(NC):
                nc.scalar.activation(coup[:, c, 0, :], coup_stage(c), ACT.Copy,
                                     scale=coup_scale[:, 0:1]).then_inc(coup_high, 1)

            def copy_turned(b, t):
                act.wait_ge(turned[1], b * NC + (t + 1))
                q0 = P * (t % TILES)
                if t % TILES == 0:
                    act.wait_ge(head_done, b * HALVES + t // TILES)
                nc.scalar.activation(probs_t[:, 4:8, q0:q0 + P],
                                     turn_ps[1].rearrange("p (k q) -> p k q", q=P), ACT.Copy)\
                  .then_inc(turned_copied[1], 1)

            with act.Fori(0, B) as b:
                act.wait_ge(qkv_done, b + 1)
                nc.scalar.activation(q_aug[0:DK, :], qkv_ps[0:DK, :], ACT.Copy).then_inc(q_ready, 1)
                nc.scalar.activation(v_t[:, :], qkv_ps[2 * DK:3 * DK, :], ACT.Copy).then_inc(v_copied, 1)
                for t in range(NC):
                    act.wait_ge(max_ready, b * NC + (t + 1))
                    if t < 2:
                        act.wait_ge(turned[1], b * NC)
                    else:
                        act.wait_ge(turned[1], b * NC + (t - 1))
                    nc.scalar.activation(probs[:, t % 2, :], score_ps[t % 2], ACT.Exp,
                                         bias=neg_max[:, t:t + 1],
                                         accum_out=row_sum[:, t:t + 1]).then_inc(probs_ready, 1)
                    if t >= 1:
                        copy_turned(b, t - 1)
                    if t == TILES:
                        act.wait_ge(head_done, b * HALVES + 1)
                        nc.scalar.activation(head_t[:, :], head_ps[0:DK, :], ACT.Copy).then_inc(head_ready, 1)
                copy_turned(b, NC - 1)
                act.wait_ge(head_done, b * HALVES + 2)
                act.wait_ge(out_done, b * NC + TILES)
                nc.scalar.activation(head_t[:, :], head_ps[0:DK, :], ACT.Copy).then_inc(head_ready, 1)

            for j in range(NCH):
                act.wait_ge(q_next[j], 1)
                nc.scalar.activation(cols(tanh_sb, CHUNKS[j]), cols(q_st[0], CHUNKS[j]), ACT.Tanh)\
                  .then_inc(tanh_ready[j], 1)
            for k, piece in enumerate(PIECES):
                nc.scalar.activation(cols(square, piece), cols(q_st[0], piece), ACT.Square)\
                  .then_inc(square_ready[k], 1)

            def tanh(stage, j, count):
                src = q_st[stage + 1] if stage + 1 < STAGES else q_raw
                act.wait_ge(q_next[j], count)
                nc.scalar.activation(cols(tanh_sb, CHUNKS[j]), cols(src, CHUNKS[j]), ACT.Tanh)\
                  .then_inc(tanh_ready[j], 1)

            def square_of(stage, k, count, step):
                if stage + 1 == STAGES:
                    act.wait_ge(clipped[k], step)
                nc.scalar.activation(cols(square, PIECES[k]), cols(q_st[(stage + 1) % STAGES], PIECES[k]),
                                     ACT.Square).then_inc(square_ready[k], 1)

            with act.Fori(0, T) as i:
                after = [act.snap(i * STAGES + (s + 2)) for s in range(STAGES)]
                step = act.snap(i + 2)
                for s in range(STAGES):
                    tanh(s, 0, after[s])
                    tanh(s, 1, after[s])
                    square_of(s, 0, after[s], step)
                    tanh(s, 2, after[s])
                    square_of(s, 1, after[s], step)

        @block.tensor
        def _(pe):
            pe.wait_ge(stack_ready, 1)
            pe.wait_ge(wo_loaded, 16)
            wo_rows = probs[:, :, :].rearrange("p a (c n) -> p (a c) n", n=T)
            for c in range(KT):
                last = nc.tensor.matmul(head_ps[0:DK, :], stack_sum[:, :], wo_rows[:, c, :],
                                        start=(c == 0), stop=(c == KT - 1))
            last.then_inc(wo_summed, 1)
            pe.wait_ge(maxes_ready, 2)
            pe.wait_ge(pool_ready, 7)
            nc.tensor.transpose(small_ps[0:1, 0:P], all_max[:, :], ident[:, :]).then_inc(max_turned, 1)
            pe.wait_ge(top_ready, 1)
            nc.tensor.matmul(small_ps[:, 0:1], ones_row[:, :], top[:, :], start=True, stop=True)\
              .then_inc(max_spread, 1)

            def scores(b, t):
                if t >= 2:
                    pe.wait_ge(probs_ready, b * NC + (t - 1))
                for h in range(HALVES):
                    last = nc.tensor.matmul(score_ps[t % 2][:, BANK * h:BANK * (h + 1)],
                                            q_aug[:, P * t:P * (t + 1)], k_aug[:, BANK * h:BANK * (h + 1)],
                                            start=True, stop=True)
                last.then_inc(scores_done, 1)

            def turn(b, t):
                pe.wait_ge(probs_ready, b * NC + (t + 1))
                for h in range(2):
                    if t == 0 and h == 0:
                        pe.wait_ge(v_ready, b + 1)
                    elif t == 0:
                        pe.wait_ge(turned_copied[h], b * NC)
                    else:
                        pe.wait_ge(turned_copied[h], b * NC + t)
                    for k in range(4):
                        kb = 4 * h + k
                        last = nc.tensor.transpose(turn_ps[h][:, P * k:P * (k + 1)],
                                                   probs[:, t % 2, P * kb:P * (kb + 1)], ident[:, :])
                    last.then_inc(turned[h], 1)

            def head(b, half):
                for h in range(2):
                    pe.wait_ge(turned_copied[h], b * NC + TILES * (half + 1))
                if half == 0:
                    pe.wait_ge(out_added, b * NC)
                else:
                    pe.wait_ge(out_added, b * NC + TILES)
                for k in range(NC):
                    last = nc.tensor.matmul(head_ps[0:DK, :], v_sb[:, k, :], probs_t[:, k, :],
                                            start=(k == 0), stop=(k == NC - 1))
                last.then_inc(head_done, 1)

            def output(b, t):
                pe.wait_ge(head_ready, b * HALVES + (t // TILES + 1))
                if t % TILES >= 2:
                    pe.wait_ge(out_added, b * NC + (t - 1))
                q0 = P * (t % TILES)
                nc.tensor.matmul(out_ps[t % 2], head_t[:, q0:q0 + P], wo_sum[:, :], start=True, stop=True)\
                  .then_inc(out_done, 1)

            with pe.Fori(0, B) as b:
                pe.wait_ge(x_loaded, b * 16 + 16)
                pe.wait_ge(probs_ready, b * NC)
                pe.wait_ge(wo_ready, 1)
                for h in range(HALVES):
                    for c in range(KT):
                        last = nc.tensor.matmul(qkv_ps[0:3 * DK, BANK * h:BANK * (h + 1)], w_qkv[:, c, :],
                                                xb[:, c, BANK * h:BANK * (h + 1)],
                                                start=(c == 0), stop=(c == KT - 1))
                last.then_inc(qkv_done, 1)
                pe.wait_ge(v_copied, b + 1)
                pe.wait_ge(turned_copied[0], b * NC)
                pe.wait_ge(q_ready, b + 1)
                pe.wait_ge(k_ready, b + 1)
                pe.wait_ge(mask_row_ready, b + 1)
                scores(b, 0)
                for c in range(NC):
                    last = nc.tensor.transpose(turn_ps[0][:, DK * c:DK * (c + 1)],
                                               v_t[:, P * c:P * (c + 1)],
                                               ident[VROW:VROW + DK, VROW:VROW + DK])
                last.then_inc(v_turned, 1)
                for t in range(1, NC):
                    scores(b, t)
                    turn(b, t - 1)
                    if t == TILES:
                        head(b, 0)
                    if t > TILES:
                        output(b, t - TILES - 1)
                output(b, TILES - 1)
                turn(b, NC - 1)
                head(b, 1)
                for t in range(TILES, NC):
                    output(b, t)

            with pe.Fori(0, T * STAGES // 2) as i:
                count = [pe.snap(i * 2 + (s + 1)) for s in range(2)]
                for s in range(2):
                    begun = [False] * NCH
                    seen = [False] * NCH
                    left = [NCH] * NCH
                    for kj, j in ORDER:
                        if not seen[kj]:
                            pe.wait_ge(parts_ready[kj], count[s])
                            seen[kj] = True
                        left[j] -= 1
                        n0, n1 = CHUNKS[j]
                        for n in range(n0, n1):
                            col = PARTS * B * (n - n0)
                            for k in range(*CHUNKS[kj]):
                                for part in range(PARTS):
                                    last = nc.tensor.matmul(
                                        ps[:, NCH * s + j, col:col + PARTS * B],
                                        coup[:, k, part, P * n:P * (n + 1)],
                                        tanh_parts[:, s, k, :, :].rearrange("p t b -> p (t b)"),
                                        start=not begun[j],
                                        stop=(left[j] == 0 and k == CHUNKS[kj][1] - 1 and part == PARTS - 1),
                                        skip_group_check=True)
                                    begun[j] = True
                        if left[j] == 0:
                            last.then_inc(product_done[j], 1)

        @block.vector
        def _(dve):
            V = nc.vector

            def axpy(out, a, factor, c, op1=ALU.add):
                return V.scalar_tensor_tensor(out=out, in0=a, scalar=factor, in1=c, op0=ALU.mult, op1=op1)

            dve.wait_ge(pool_ready, 7)
            V.tensor_reduce(stack_sum[:, :], stack[:, :, :].rearrange("p i d -> p d i"), AX.X, ALU.add)\
             .then_inc(stack_ready, 1)
            dve.wait_ge(wo_summed, 1)
            V.tensor_copy(wo_sum[:, :], head_ps[0:DK, :]).then_inc(wo_ready, 1)
            dve.wait_ge(coup_loaded, 16 * NC)
            for c in range(NC):
                last = V.tensor_reduce(col_max[:, c:c + 1], coup_stage(c), AX.X, ALU.max,
                                       apply_absolute_value=True)
            last.then_inc(maxes_ready, 1)
            dve.wait_ge(maxes_ready, 1)
            V.tensor_reduce(all_max[:, :], col_max[:, :], AX.X, ALU.max).then_inc(maxes_ready, 1)
            dve.wait_ge(max_turned, 1)
            V.tensor_reduce(top[:, :], small_ps[0:1, 0:P], AX.X, ALU.max).then_inc(top_ready, 1)
            dve.wait_ge(max_spread, 1)
            V.tensor_scalar(all_max[:, :], small_ps[:, 0:1], 2.0 ** -100, 2.0 ** 100, ALU.max, ALU.min)\
             .then_inc(setup, 1)
            dve.wait_ge(setup, 1)
            V.tensor_scalar(power[:, :].bitcast(I32), all_max[:, :].bitcast(I32), 0x7f800000, None,
                            ALU.bitwise_and).then_inc(setup, 1)
            dve.wait_ge(setup, 2)
            V.reciprocal(inv_power[:, :], power[:, :]).then_inc(setup, 1)
            dve.wait_ge(setup, 3)
            V.tensor_scalar(coup_scale[:, :], inv_power[:, :], 2.0 ** COUP_EXP, None, ALU.mult)\
             .then_inc(scale_ready, 1)
            for s in range(STAGES):
                last = V.tensor_scalar(step_scale[:, s:s + 1], power[:, :], 2.0 ** -COUP_EXP,
                                       STEP[s] / TANH_SCALE, ALU.mult, ALU.mult)
            last.then_inc(setup, 1)
            dve.wait_ge(scale_ready, 1)
            for c in range(NC):
                dve.wait_ge(coup_high, c + 1)
                V.scalar_tensor_tensor(out=coup[:, c, 1, :], in0=coup_stage(c), scalar=coup_scale[:, 0:1],
                                       in1=coup[:, c, 0, :], op0=ALU.mult, op1=ALU.subtract)\
                 .then_inc(coup_low, 1)

            def row_max(b, t):
                dve.wait_ge(scores_done, b * NC + (t + 1))
                V.tensor_reduce(neg_max[:, t:t + 1], score_ps[t % 2], AX.X, ALU.max, negate=True)\
                 .then_inc(max_ready, 1)

            def copy_turned_low(b, t):
                dve.wait_ge(turned[0], b * NC + (t + 1))
                q0 = P * (t % TILES)
                if t % TILES == 0:
                    dve.wait_ge(head_done, b * HALVES + t // TILES)
                V.tensor_copy(probs_t[:, 0:4, q0:q0 + P], turn_ps[0].rearrange("p (k q) -> p k q", q=P))\
                 .then_inc(turned_copied[0], 1)

            def scale_rows(b, half):
                r = slice(TILES * half, TILES * (half + 1))
                dve.wait_ge(probs_ready, b * NC + TILES * (half + 1))
                V.reciprocal(inv_sum[:, r], row_sum[:, r]).then_inc(inv_ready, 1)
                dve.wait_ge(inv_ready, b * HALVES + (half + 1))
                V.tensor_tensor(row_scale[:, r].rearrange("p (c o) -> p c o", o=1),
                                inv_sum[:, r].rearrange("p (c o) -> p c o", o=1),
                                cond_sb[:, r, bass.ds(b, 1)], ALU.mult).then_inc(row_scale_ready, 1)

            def add_output(b, t):
                dve.wait_ge(out_done, b * NC + (t + 1))
                dve.wait_ge(row_scale_ready, b * HALVES + (t // TILES + 1))
                column = drive[:, 0:T, bass.ds(b + B * t, 1)].rearrange("p t o -> p (t o)")
                axpy(column, out_ps[t % 2], row_scale[:, t:t + 1], column).then_inc(out_added, 1)

            dve.wait_ge(consts_loaded, 16 * 5)
            dve.wait_ge(drive_loaded, 16 * 8)
            with dve.Fori(0, B) as b:
                dve.wait_ge(qkv_done, b + 1)
                dve.wait_ge(mask_loaded, b * 16 + 16)
                axpy(k_aug[0:DK, :], qkv_ps[DK:2 * DK, :], DK ** -0.5, mask_bc[0:DK, :], ALU.mult)\
                    .then_inc(k_ready, 1)
                V.tensor_scalar(k_aug[DK:DK + 1, :], mask_bc[DK:DK + 1, :], -MASKED, MASKED, ALU.mult, ALU.add)\
                 .then_inc(mask_row_ready, 1)
                dve.wait_ge(v_turned, b + 1)
                V.tensor_copy(v_sb[:, :, :].rearrange("p c d -> p (c d)"), turn_ps[0][:, 0:NC * DK])\
                 .then_inc(v_ready, 1)
                for t in range(NC):
                    row_max(b, t)
                    if t >= 1:
                        copy_turned_low(b, t - 1)
                    if t == TILES:
                        scale_rows(b, 0)
                    if t > TILES:
                        add_output(b, t - TILES - 1)
                add_output(b, TILES - 1)
                copy_turned_low(b, NC - 1)
                scale_rows(b, 1)
                for t in range(TILES, NC):
                    add_output(b, t)

            full = (0, NC)
            first = 4
            V.tensor_copy(q_st[0][:, :], cond_sb[:, :, :].rearrange("p c b -> p (c b)")).then_inc(setup, 1)
            V.tensor_scalar(p_st[:, :], cond_sb[:, :, :].rearrange("p c b -> p (c b)"), -SHIFT, None, ALU.add)\
             .then_inc(setup, 1)
            V.memset(z[:, :], 0.0).then_inc(setup, 1)
            dve.wait_ge(setup, first + 3)
            for c in range(NC):
                last = V.tensor_scalar(cols(bias_b, (c, c + 1)), cols(z, (c, c + 1)), bias_sb[:, c:c + 1],
                                       -SHIFT, ALU.add, ALU.add)
            last.then_inc(setup, 1)
            dve.wait_ge(setup, first + 4)
            for j in range(NCH):
                V.engine_nop().then_inc(q_next[j], 1)
            V.tensor_tensor(drive_b[:, :], drive[:, 0, :], bias_b[:, :], ALU.add).then_inc(drive_b_ready, 1)
            dve.wait_ge(drive_b_ready, 1)
            V.tensor_tensor(drive_p[:, :], drive_b[:, :], p_st[:, :], ALU.subtract).then_inc(drive_p_ready, 1)
            V.engine_nop().then_inc(p_ready, 1)

            def split_high(parity, j, count):
                dve.wait_ge(tanh_ready[j], count)
                c0, c1 = CHUNKS[j]
                V.tensor_scalar(tanh_parts[:, parity, c0:c1, 0, :], by_block(tanh_sb, CHUNKS[j]),
                                TANH_SCALE, None, ALU.mult).then_inc(high_ready[j], 1)

            def split_low(parity, j, count):
                dve.wait_ge(high_ready[j], count)
                c0, c1 = CHUNKS[j]
                axpy(tanh_parts[:, parity, c0:c1, 1, :], by_block(tanh_sb, CHUNKS[j]), TANH_SCALE,
                     tanh_parts[:, parity, c0:c1, 0, :], ALU.subtract).then_inc(parts_ready[j], 1)

            def z_of_first(k, step):
                dve.wait_ge(drive_p_ready, step)
                dve.wait_ge(clipped[k], step)
                axpy(cols(z, PIECES[k]), cols(drive_p, PIECES[k]), DT / 2, cols(q_st[0], PIECES[k]))\
                    .then_inc(z_ready[k], 1)

            def cubic_of(stage, k, count):
                dve.wait_ge(square_ready[k], count)
                q = cols(q_st[stage], PIECES[k])
                V.scalar_tensor_tensor(out=cols(cubic, PIECES[k]), in0=cols(square, PIECES[k]), scalar=-3.0,
                                       in1=q, op0=ALU.add, op1=ALU.mult).then_inc(cubic_ready[k], 1)

            def base_of(stage, k, count):
                dve.wait_ge(cubic_ready[k], count)
                axpy(cols(base, PIECES[k]), cols(cubic, PIECES[k]), -STEP[stage] / 3,
                     cols([z, z2, z3, z][stage], PIECES[k])).then_inc(base_ready[k], 1)

            for k in range(len(PIECES)):
                V.engine_nop().then_inc(clipped[k], 1)
                z_of_first(k, 1)
            for j in range(NCH):
                split_high(0, j, 1)
                split_low(0, j, 1)
            for k in range(len(PIECES)):
                dve.wait_ge(z_ready[k], 1)
                cubic_of(0, k, 1)
                base_of(0, k, 1)

            with dve.Fori(0, T) as i:
                now = [dve.snap(i * STAGES + (s + 1)) for s in range(STAGES + 1)]
                step = dve.snap(i + 1)
                next_step = dve.snap(i + 2)

                def add_high(s, j):
                    if j != 1:
                        dve.wait_ge(base_ready[j // 2], now[s])
                    dve.wait_ge(product_done[j], now[s])
                    axpy(by_block(half_sum, CHUNKS[j]), product(s, j, 0), step_scale[:, s:s + 1],
                         by_block(base, CHUNKS[j])).then_inc(half_ready[j], 1)

                def add_low(s, j):
                    dve.wait_ge(half_ready[j], now[s])
                    out = q_st[s + 1] if s + 1 < STAGES else q_raw
                    axpy(by_block(out, CHUNKS[j]), product(s, j, 1), step_scale[:, s:s + 1],
                         by_block(half_sum, CHUNKS[j])).then_inc(q_next[j], 1)

                def clip_q(k):
                    dve.wait_ge(q_next[k + 1], now[STAGES])
                    V.tensor_scalar(cols(q_st[0], PIECES[k]), cols(q_raw, PIECES[k]), -CLAMP, CLAMP,
                                    ALU.max, ALU.min).then_inc(clipped[k], 1)

                def z_of_last(k):
                    dve.wait_ge(x_third_ready, step)
                    dve.wait_ge(q_next[k + 1], now[3])
                    axpy(cols(z, PIECES[k]), cols(q_st[3], PIECES[k]), 1.0 / 3, cols(x_third, PIECES[k]))\
                        .then_inc(z4_ready[k], 1)

                def g_of(s):
                    if s == 0:
                        dve.wait_ge(p_ready, step)
                        dve.wait_ge(clipped[1], step)
                        p_now = p_st
                    else:
                        dve.wait_ge(p_mid_ready[s - 1], step)
                        p_now = p_mid
                    axpy(g[s][:, :], p_now[:, :], -BETA, q_st[s][:, :]).then_inc(g_ready[s], 1)

                def p_of(s):
                    dve.wait_ge(g_ready[s], step)
                    axpy(p_mid[:, :], g[s][:, :], STEP[s] * EPS, p_st[:, :]).then_inc(p_mid_ready[s], 1)

                def z_of_second():
                    dve.wait_ge(g_ready[0], step)
                    dve.wait_ge(z_ready[1], step)
                    axpy(z2[:, :], g[0][:, :], -DT * DT / 4 * EPS, z[:, :]).then_inc(z2_ready, 1)

                def y_of():
                    axpy(y_mid[:, :], z[:, :], 2.0, q_st[0][:, :], ALU.subtract).then_inc(y_ready, 1)

                def x_first():
                    axpy(x_sum[:, :], q_st[0][:, :], -2.0, z[:, :]).then_inc(x_sum_ready[0], 1)

                def look_ahead():
                    V.tensor_tensor(drive_b[:, :], drive[:, bass.ds(i + 1, 1), :].rearrange("p o c -> p (o c)"),
                                    bias_b[:, :], ALU.add).then_inc(drive_b_ready, 1)

                def z_of_third():
                    dve.wait_ge(g_ready[1], step)
                    dve.wait_ge(y_ready, step)
                    axpy(z3[:, :], g[1][:, :], -DT * DT / 2 * EPS, y_mid[:, :]).then_inc(z3_ready, 1)

                def x_second():
                    dve.wait_ge(x_sum_ready[0], step)
                    V.tensor_tensor(x_sum2[:, :], x_sum[:, :], q_st[1][:, :], ALU.add)\
                     .then_inc(x_sum_ready[1], 1)

                def g_sum_first():
                    axpy(g_sum[:, :], g[1][:, :], 2.0, g[0][:, :]).then_inc(g_sum_ready[0], 1)

                def x_q2():
                    dve.wait_ge(x_sum_ready[1], step)
                    axpy(x_sum[:, :], q_st[2][:, :], 2.0, x_sum2[:, :]).then_inc(x_sum_ready[2], 1)

                def x_g2():
                    dve.wait_ge(g_ready[2], step)
                    dve.wait_ge(x_sum_ready[2], step)
                    axpy(x_sum2[:, :], g[2][:, :], -DT * DT / 2 * EPS, x_sum[:, :]).then_inc(x_sum_ready[3], 1)

                def x_divide():
                    dve.wait_ge(x_sum_ready[3], step)
                    V.tensor_scalar(x_third[:, :], x_sum2[:, :], 1.0 / 3, None, ALU.mult)\
                     .then_inc(x_third_ready, 1)

                def g_sum_second():
                    dve.wait_ge(g_sum_ready[0], step)
                    axpy(g[0][:, :], g[2][:, :], 2.0, g_sum[:, :]).then_inc(g_sum_ready[1], 1)

                def g_sum_third():
                    dve.wait_ge(g_ready[3], step)
                    dve.wait_ge(g_sum_ready[1], step)
                    V.tensor_tensor(g_sum[:, :], g[0][:, :], g[3][:, :], ALU.add).then_inc(g_sum_ready[2], 1)

                def p_next():
                    dve.wait_ge(g_sum_ready[2], step)
                    axpy(p_raw[:, :], g_sum[:, :], DT / 6 * EPS, p_st[:, :]).then_inc(p_raw_ready, 1)

                def clip_p():
                    dve.wait_ge(p_raw_ready, step)
                    V.tensor_scalar(p_st[:, :], p_raw[:, :], -CLAMP - SHIFT, CLAMP - SHIFT, ALU.max, ALU.min)\
                     .then_inc(p_ready, 1)

                def drive_less_p():
                    dve.wait_ge(p_ready, next_step)
                    dve.wait_ge(drive_b_ready, next_step)
                    V.tensor_tensor(drive_p[:, :], drive_b[:, :], p_st[:, :], ALU.subtract)\
                     .then_inc(drive_p_ready, 1)

                def trace():
                    dve.wait_ge(clipped[1], next_step)
                    at = drive[:, bass.ds(i, 1), :].rearrange("p o c -> p (o c)")
                    V.tensor_tensor(at, at, q_st[0][:, :], ALU.add).then_inc(traced, 1)

                side = [
                    [lambda: g_of(0), z_of_second, lambda: p_of(0), y_of, x_first, look_ahead],
                    [lambda: g_of(1), z_of_third, lambda: p_of(1), x_second, g_sum_first],
                    [lambda: g_of(2), x_q2, x_g2, lambda: p_of(2), x_divide, g_sum_second],
                    [lambda: g_of(3), g_sum_third, p_next, clip_p, drive_less_p],
                ]
                for s in range(STAGES):
                    last_stage = s == STAGES - 1
                    after = (s + 1) % STAGES
                    parity = (s + 1) % 2
                    add_high(s, 0)
                    side[s][0]()
                    add_low(s, 0)
                    side[s][1]()
                    add_high(s, 1)
                    split_high(parity, 0, now[s + 1])
                    add_low(s, 1)
                    split_low(parity, 0, now[s + 1])
                    side[s][2]()
                    if last_stage:
                        clip_q(0)
                    side[s][3]()
                    split_high(parity, 1, now[s + 1])
                    side[s][4]()
                    split_low(parity, 1, now[s + 1])
                    if s == 2:
                        side[s][5]()
                    if last_stage:
                        z_of_first(0, next_step)
                    if s == 2:
                        z_of_last(0)
                    cubic_of(after, 0, now[s + 1])
                    add_high(s, 2)
                    base_of(after, 0, now[s + 1])
                    add_low(s, 2)
                    if s == 0:
                        side[s][5]()
                    if last_stage:
                        clip_q(1)
                    if s == 2:
                        z_of_last(1)
                    split_high(parity, 2, now[s + 1])
                    if last_stage:
                        z_of_first(1, next_step)
                    split_low(parity, 2, now[s + 1])
                    cubic_of(after, 1, now[s + 1])
                    if last_stage:
                        trace()
                    base_of(after, 1, now[s + 1])


def kernel(x, cond_2048, L0_cond_Wq, L0_cond_Wk, L0_cond_Wv, L0_cond_Wo, L1_cond_coupling, L1_cond_bias):
    import numpy as np
    import concourse.bacc as bacc
    from concourse.bass_utils import run_bass_kernel_spmd

    x, cond, coupling, bias = (np.asarray(a) for a in (x, cond_2048, L1_cond_coupling, L1_cond_bias))
    arrays = {
        "x": x,
        "x_pt": x.reshape(B, T, NC, P).transpose(3, 1, 2, 0).reshape(P, T, COLS),
        "cond": cond,
        "cond_p": cond.reshape(B, NC, P).transpose(2, 1, 0),
        "wq": np.asarray(L0_cond_Wq)[1],
        "wk": np.asarray(L0_cond_Wk)[1],
        "wv": np.asarray(L0_cond_Wv)[1],
        "wo": np.asarray(L0_cond_Wo),
        "coupling_t": coupling.T,
        "bias_p": bias.reshape(NC, P).T,
    }
    arrays = {k: np.ascontiguousarray(a) for k, a in arrays.items()}
    nc = bacc.Bacc("TRN2", target_bir_lowering=False, num_devices=1,
                   dynamic_dma_scratch_size=1024)
    args = [nc.dram_tensor(f"in_{k}", a.shape, mybir.dt.from_np(a.dtype), kind="ExternalInput").ap()
            for k, a in arrays.items()]
    out = nc.dram_tensor("out_pt", (P, T, COLS), F32, kind="ExternalOutput").ap()
    build(nc, *args, out)
    r = run_bass_kernel_spmd(nc, [{f"in_{k}": a for k, a in arrays.items()}], core_ids=[0])
    got = np.asarray(r.results[0]["out_pt"])
    return np.ascontiguousarray(got.reshape(P, T, NC, B).transpose(3, 1, 2, 0).reshape(B, T, N))
```

```python
import concourse.bass as bass
from concourse import mybir
from contextlib import ExitStack

F32 = mybir.dt.float32
F16 = mybir.dt.float16
I32 = mybir.dt.int32
ALU = mybir.AluOpType
ACT = mybir.ActivationFunctionType
AX = mybir.AxisListType

P = 128
B = 8
T = 512
N = 1024
NC = N // P
KT = T // P
DK = 32
VROW = 2 * DK
HROW = 3 * DK
COLS = NC * B
BANK = 512
NBANK = 8
HALVES = N // BANK
TILES = BANK // P
MASKED = -1e30

DT, EPS, ALPHA, BETA, CLAMP = 0.01, 0.08, 0.7, 0.8, 20.0
SHIFT = ALPHA / BETA
STAGES = 4
STEPS = T
RISE = DT / 2 * EPS
STEP = [DT / 2, DT / 2, DT, DT / 6]
THIRD = 5592405 / 2 ** 24

G1 = [1 - BETA * RISE, 1.0, 0.0]
G2 = [1 - BETA * RISE * G1[0], -BETA * RISE * G1[1], 1.0]
G3 = [1 - 2 * BETA * RISE * G2[0], -2 * BETA * RISE * G2[1], -2 * BETA * RISE * G2[2]]
P_SUM = [(k == 0) + 2 * G1[k] + 2 * G2[k] + G3[k] for k in range(3)]
Q_SUM = [-DT * RISE * G2[0], 1 - DT * RISE * G2[1], 2 - DT * RISE * G2[2]]

CHUNKS = [(0, 1), (1, 3), (3, 6), (6, 8)]
NCH = len(CHUNKS)
ORDER = [(0, 2), (0, 0), (0, 1), (1, 2), (1, 3), (1, 0), (1, 1), (2, 0), (2, 1), (3, 0), (3, 1), (3, 2),
         (2, 2), (0, 3), (3, 3), (2, 3)]
PARTS = 2
MOVING = 32
UNROLLED = 2
TANH_SCALE = 4096.0
COUP_EXP = 14
STORE_STEPS = 32


def build(nc, x, x_pt, cond, cond_p, wq, wk, wv, wo, coupling_t, bias_p, out_pt):
    ctx = ExitStack()
    with ctx:
        def sb(name, shape, dt=F32):
            return ctx.enter_context(nc.sbuf_tensor(name, shape, dt))

        def sem(name):
            return ctx.enter_context(nc.semaphore(name))

        drive = sb("drive", [P, T + 2, COLS])
        steps = drive[:, 1:1 + T, :]
        drive_cols = drive[:, :, :].rearrange("p t c -> p (t c)")
        coup = sb("coup", [P, NC, PARTS, N], F16)
        tanh_parts = sb("tanh_parts", [P, 2, NC, MOVING], F16)

        xb = sb("xb", [P, KT, N])
        w_qkv = sb("w_qkv", [P, KT, 3 * DK])
        qv = sb("qv", [P, N])
        km = sb("km", [P, N])
        q_aug = qv[0:DK + 1, :]
        v_t = qv[VROW:VROW + DK, :]
        head_t = qv[HROW:HROW + DK, 0:BANK]
        wo_sum = qv[HROW:HROW + DK, BANK:BANK + T]
        k_aug = km[0:DK + 1, :]
        mask_bc = km[VROW:VROW + DK + 1, :]
        v_sb = sb("v_sb", [P, NC, DK])
        probs = sb("probs", [P, 2, N])
        probs_t = sb("probs_t", [P, NC, BANK])
        neg_max = sb("neg_max", [P, NC])
        row_sum = sb("row_sum", [P, NC])
        inv_sum = sb("inv_sum", [P, NC])
        row_scale = sb("row_scale", [P, NC])
        ident = sb("ident", [P, P])
        stack = sb("stack", [P, P // DK, DK])
        stack_sum = sb("stack_sum", [P, DK])
        ones_row = sb("ones_row", [1, P])

        col_max = sb("col_max", [P, NC])
        all_max = sb("all_max", [P, 1])
        top = sb("top", [1, 1])
        power = sb("power", [P, 1])
        inv_power = sb("inv_power", [P, 1])
        coup_scale = sb("coup_scale", [P, 1])

        cond_sb = sb("cond_sb", [P, NC, B])
        bias_sb = sb("bias_sb", [P, NC])
        step_scale = sb("step_scale", [P, STAGES])
        q_st = [sb(f"q_st{s}", [P, COLS]) for s in range(STAGES)]
        q_raw = sb("q_raw", [P, COLS])
        half_sum = sb("half_sum", [P, COLS])
        tanh_sb = sb("tanh_sb", [P, COLS])
        square = sb("square", [P, COLS])
        square0 = sb("square0", [P, COLS])
        cubic = sb("cubic", [P, COLS])
        base = sb("base", [P, COLS])
        z = sb("z", [P, COLS])
        z2 = sb("z2", [P, COLS])
        z3 = sb("z3", [P, COLS])
        p_st = sb("p_st", [P, COLS])
        p_raw = sb("p_raw", [P, COLS])
        bias_b = sb("bias_b", [P, COLS])
        drive_b = sb("drive_b", [P, COLS])
        drive_p = sb("drive_p", [P, COLS])
        g0 = sb("g0", [P, COLS])
        y = sb("y", [P, COLS])
        y_less = sb("y_less", [P, COLS])
        q_share = sb("q_share", [P, COLS])
        rise = [sb(f"rise{k}", [P, COLS]) for k in (1, 2)]
        q_sum = [sb(f"q_sum{k}", [P, COLS]) for k in range(3)]
        p_sum = [sb(f"p_sum{k}", [P, COLS]) for k in range(4)]
        z_rest = sb("z_rest", [P, COLS])

        ps = ctx.enter_context(nc.psum_tensor("ps", [P, NBANK, BANK], F32))
        score_ps = [ps[:, 0:2, :].rearrange("p a n -> p (a n)"), ps[:, 2:4, :].rearrange("p a n -> p (a n)")]
        turn_ps = [ps[:, 4, :], ps[:, 5, :]]
        head_ps = ps[:, 6, :]
        out_ps = [ps[:, 7, :], ps[:, 6, :]]
        qkv_ps = score_ps[0]
        small_ps = ps[:, 7, :]

        coup_loaded = sem("coup_loaded")
        consts_loaded = sem("consts_loaded")
        wo_loaded = sem("wo_loaded")
        drive_loaded = sem("drive_loaded")
        x_loaded = sem("x_loaded")
        mask_loaded = sem("mask_loaded")
        stored = sem("stored")

        pool_ready = sem("pool_ready")
        stack_ready = sem("stack_ready")
        wo_summed = sem("wo_summed")
        wo_ready = sem("wo_ready")
        maxes_ready = sem("maxes_ready")
        max_turned = sem("max_turned")
        top_ready = sem("top_ready")
        max_spread = sem("max_spread")
        scale_ready = sem("scale_ready")
        coup_high = sem("coup_high")
        coup_low = sem("coup_low")
        setup = sem("setup")

        qkv_done = sem("qkv_done")
        q_ready = sem("q_ready")
        k_ready = sem("k_ready")
        v_copied = sem("v_copied")
        mask_row_ready = sem("mask_row_ready")
        v_turned = sem("v_turned")
        v_ready = sem("v_ready")
        scores_done = sem("scores_done")
        max_ready = sem("max_ready")
        probs_ready = sem("probs_ready")
        turned = [sem("turned0"), sem("turned1")]
        turned_copied = [sem("turned_copied0"), sem("turned_copied1")]
        head_done = sem("head_done")
        head_ready = sem("head_ready")
        inv_ready = sem("inv_ready")
        row_scale_ready = sem("row_scale_ready")
        out_done = sem("out_done")
        out_added = sem("out_added")

        product_done = [sem(f"product_done{j}") for j in range(NCH)]
        half_ready = [sem(f"half_ready{j}") for j in range(NCH)]
        q_next = [sem(f"q_next{j}") for j in range(NCH)]
        tanh_ready = [sem(f"tanh_ready{j}") for j in range(NCH)]
        high_ready = [sem(f"high_ready{j}") for j in range(NCH)]
        parts_ready = [sem(f"parts_ready{j}") for j in range(NCH)]
        square_ready = sem("square_ready")
        square0_ready = sem("square0_ready")
        cubic_ready = sem("cubic_ready")
        base_ready = sem("base_ready")
        clipped = sem("clipped")
        p_ready = sem("p_ready")
        drive_p_ready = sem("drive_p_ready")
        q_share_ready = sem("q_share_ready")
        traced = sem("traced")

        def cols(t, blocks):
            return t[:, B * blocks[0]:B * blocks[1]]

        def by_block(t, blocks):
            return cols(t, blocks).rearrange("p (c b) -> p c b", b=B)

        def product(stage, j, part):
            w = CHUNKS[j][1] - CHUNKS[j][0]
            return ps[:, NCH * (stage % 2) + j, 0:w * MOVING].rearrange(
                "p (c m) -> p c m", m=MOVING)[:, :, B * part:B * (part + 1)]

        def tanh_part(parity, j, part):
            return tanh_parts[:, parity, CHUNKS[j][0]:CHUNKS[j][1], B * part:B * (part + 1)]

        def coup_stage(c):
            half = probs_t[:, :, :].rearrange("p a n -> p (a n)")[:, (c - KT) * N:(c - KT + 1) * N]
            return xb[:, c, :] if c < KT else half

        block = ctx.enter_context(nc.Block())

        @block.sync
        def _(sp):
            for c in range(NC):
                sp.dma_start(coup_stage(c), coupling_t[P * c:P * (c + 1), :]).then_inc(coup_loaded, 16)
            sp.dma_start(cond_sb[:, :, :], cond_p).then_inc(consts_loaded, 16)
            sp.dma_start(bias_sb[:, :], bias_p).then_inc(consts_loaded, 16)
            for i, w in enumerate((wq, wk, wv)):
                sp.dma_start(w_qkv[:, :, DK * i:DK * (i + 1)],
                             w.rearrange("(c p) d -> p c d", p=P)).then_inc(consts_loaded, 16)
            sp.wait_ge(coup_high, NC)
            sp.wait_ge(coup_low, NC)
            with sp.Fori(0, B) as b:
                sp.wait_ge(qkv_done, b)
                sp.dma_start(xb[:, :, :], x[bass.ds(b, 1), :, :].rearrange("o (c p) n -> p (o c) n", p=P))\
                  .then_inc(x_loaded, 16)
                sp.wait_ge(k_ready, b)
                sp.wait_ge(mask_row_ready, b)
                sp.dma_start(mask_bc[:, :], cond[bass.ds(b, 1), :].broadcast_to([DK + 1, N]))\
                  .then_inc(mask_loaded, 16)
            with sp.Fori(0, T // STORE_STEPS) as i:
                sp.wait_ge(traced, i * STORE_STEPS + (1 + STORE_STEPS))
                sp.dma_start(out_pt[:, bass.ds(i * STORE_STEPS, STORE_STEPS), :],
                             steps[:, bass.ds(i * STORE_STEPS, STORE_STEPS), :]).then_inc(stored, 16)
            sp.wait_ge(stored, 16 * (T // STORE_STEPS))

        @block.gpsimd
        def _(pool):
            nc.gpsimd.memset(ident[:, :], 0.0).then_inc(pool_ready, 1)
            pool.wait_ge(pool_ready, 1)
            nc.gpsimd.memset(stack[:, :, :], 0.0).then_inc(pool_ready, 1)
            pool.wait_ge(pool_ready, 2)
            nc.gpsimd.memset(ones_row[:, :], 1.0).then_inc(pool_ready, 1)
            pool.wait_ge(pool_ready, 3)
            nc.gpsimd.memset(q_aug[DK:DK + 1, :], 1.0).then_inc(pool_ready, 1)
            pool.wait_ge(pool_ready, 4)
            nc.gpsimd.memset(drive[:, 0, :], 0.0).then_inc(pool_ready, 1)
            pool.wait_ge(pool_ready, 5)
            nc.gpsimd.memset(drive[:, 1 + T, :], 0.0).then_inc(pool_ready, 1)
            pool.wait_ge(pool_ready, 6)
            nc.gpsimd.affine_select(out=ident[:, :], in_=ident[:, :], compare_op=ALU.not_equal, fill=1.0,
                                    base=0, pattern=[[-1, P]], channel_multiplier=1).then_inc(pool_ready, 1)
            pool.wait_ge(pool_ready, 7)
            nc.gpsimd.affine_select(out=stack[:, :, :], in_=stack[:, :, :], compare_op=ALU.not_equal,
                                    fill=1.0, base=0, pattern=[[-DK, P // DK], [-1, DK]],
                                    channel_multiplier=1).then_inc(pool_ready, 1)

        @block.scalar
        def _(act):
            act.dma_start(probs[:, :, :].rearrange("p a (c n) -> p (a c) n", n=T),
                          wo.rearrange("(c p) n -> p c n", p=P)).then_inc(wo_loaded, 16)
            for i in range(8):
                s = slice(i * T // 8, (i + 1) * T // 8)
                act.dma_start(steps[:, s, :], x_pt[:, s, :]).then_inc(drive_loaded, 16)
            act.wait_ge(scale_ready, 1)
            for c in range(NC):
                nc.scalar.activation(coup[:, c, 0, :], coup_stage(c), ACT.Copy,
                                     scale=coup_scale[:, 0:1]).then_inc(coup_high, 1)

            def copy_turned(b, t):
                act.wait_ge(turned[1], b * NC + (t + 1))
                q0 = P * (t % TILES)
                if t % TILES == 0:
                    act.wait_ge(head_done, b * HALVES + t // TILES)
                nc.scalar.activation(probs_t[:, 4:8, q0:q0 + P],
                                     turn_ps[1].rearrange("p (k q) -> p k q", q=P), ACT.Copy)\
                  .then_inc(turned_copied[1], 1)

            with act.Fori(0, B) as b:
                act.wait_ge(qkv_done, b + 1)
                nc.scalar.activation(q_aug[0:DK, :], qkv_ps[0:DK, :], ACT.Copy).then_inc(q_ready, 1)
                nc.scalar.activation(v_t[:, :], qkv_ps[2 * DK:3 * DK, :], ACT.Copy).then_inc(v_copied, 1)
                for t in range(NC):
                    act.wait_ge(max_ready, b * NC + (t + 1))
                    if t < 2:
                        act.wait_ge(turned[1], b * NC)
                    else:
                        act.wait_ge(turned[1], b * NC + (t - 1))
                    nc.scalar.activation(probs[:, t % 2, :], score_ps[t % 2], ACT.Exp,
                                         bias=neg_max[:, t:t + 1],
                                         accum_out=row_sum[:, t:t + 1]).then_inc(probs_ready, 1)
                    if t >= 1:
                        copy_turned(b, t - 1)
                    if t == TILES:
                        act.wait_ge(head_done, b * HALVES + 1)
                        nc.scalar.activation(head_t[:, :], head_ps[0:DK, :], ACT.Copy).then_inc(head_ready, 1)
                copy_turned(b, NC - 1)
                act.wait_ge(head_done, b * HALVES + 2)
                act.wait_ge(out_done, b * NC + TILES)
                nc.scalar.activation(head_t[:, :], head_ps[0:DK, :], ACT.Copy).then_inc(head_ready, 1)

            def tanh(q, j, count):
                act.wait_ge(q_next[j], count)
                nc.scalar.activation(cols(tanh_sb, CHUNKS[j]), cols(q, CHUNKS[j]), ACT.Tanh)\
                  .then_inc(tanh_ready[j], 1)

            def split_high(parity, j, count):
                act.wait_ge(tanh_ready[j], count)
                nc.scalar.activation(tanh_part(parity, j, 0), by_block(tanh_sb, CHUNKS[j]), ACT.Copy,
                                     scale=TANH_SCALE).then_inc(high_ready[j], 1)

            for j in range(NCH):
                tanh(q_st[0], j, 1)
                split_high(0, j, 1)

            with act.Fori(1, 1 + STAGES * STEPS, STAGES * UNROLLED) as now:
                for u in range(STAGES * UNROLLED):
                    s, parity = u % STAGES, (u + 1) % 2
                    made = act.snap(now + 1)
                    q = q_st[s + 1] if s + 1 < STAGES else q_raw
                    tanh(q, 0, made)
                    tanh(q, 1, made)
                    split_high(parity, 0, made)
                    split_high(parity, 1, made)
                    tanh(q, 2, made)
                    split_high(parity, 2, made)
                    tanh(q, 3, made)
                    if s + 1 < STAGES:
                        nc.scalar.activation(square[:, :], q_st[s + 1][:, :], ACT.Square)\
                          .then_inc(square_ready, 2 if s == 0 else 1)
                    split_high(parity, 3, made)
                    if s == 0:
                        nc.scalar.activation(q_share[:, :], q_st[0][:, :], ACT.Copy, scale=1 - THIRD)\
                          .then_inc(q_share_ready, STAGES)
                    now = made

        @block.tensor
        def _(pe):
            pe.wait_ge(stack_ready, 1)
            pe.wait_ge(wo_loaded, 16)
            wo_rows = probs[:, :, :].rearrange("p a (c n) -> p (a c) n", n=T)
            for c in range(KT):
                last = nc.tensor.matmul(head_ps[0:DK, :], stack_sum[:, :], wo_rows[:, c, :],
                                        start=(c == 0), stop=(c == KT - 1))
            last.then_inc(wo_summed, 1)
            pe.wait_ge(maxes_ready, 2)
            pe.wait_ge(pool_ready, 8)
            nc.tensor.transpose(small_ps[0:1, 0:P], all_max[:, :], ident[:, :]).then_inc(max_turned, 1)
            pe.wait_ge(top_ready, 1)
            nc.tensor.matmul(small_ps[:, 0:1], ones_row[:, :], top[:, :], start=True, stop=True)\
              .then_inc(max_spread, 1)

            def scores(b, t):
                if t >= 2:
                    pe.wait_ge(probs_ready, b * NC + (t - 1))
                for h in range(HALVES):
                    last = nc.tensor.matmul(score_ps[t % 2][:, BANK * h:BANK * (h + 1)],
                                            q_aug[:, P * t:P * (t + 1)], k_aug[:, BANK * h:BANK * (h + 1)],
                                            start=True, stop=True)
                last.then_inc(scores_done, 1)

            def turn(b, t):
                pe.wait_ge(probs_ready, b * NC + (t + 1))
                for h in range(2):
                    if t == 0 and h == 0:
                        pe.wait_ge(v_ready, b + 1)
                    elif t == 0:
                        pe.wait_ge(turned_copied[h], b * NC)
                    else:
                        pe.wait_ge(turned_copied[h], b * NC + t)
                    for k in range(4):
                        kb = 4 * h + k
                        last = nc.tensor.transpose(turn_ps[h][:, P * k:P * (k + 1)],
                                                   probs[:, t % 2, P * kb:P * (kb + 1)], ident[:, :])
                    last.then_inc(turned[h], 1)

            def head(b, half):
                for h in range(2):
                    pe.wait_ge(turned_copied[h], b * NC + TILES * (half + 1))
                if half == 0:
                    pe.wait_ge(out_added, b * NC)
                else:
                    pe.wait_ge(out_added, b * NC + TILES)
                for k in range(NC):
                    last = nc.tensor.matmul(head_ps[0:DK, :], v_sb[:, k, :], probs_t[:, k, :],
                                            start=(k == 0), stop=(k == NC - 1))
                last.then_inc(head_done, 1)

            def output(b, t):
                pe.wait_ge(head_ready, b * HALVES + (t // TILES + 1))
                if t % TILES >= 2:
                    pe.wait_ge(out_added, b * NC + (t - 1))
                q0 = P * (t % TILES)
                nc.tensor.matmul(out_ps[t % 2], head_t[:, q0:q0 + P], wo_sum[:, :], start=True, stop=True)\
                  .then_inc(out_done, 1)

            with pe.Fori(0, B) as b:
                pe.wait_ge(x_loaded, b * 16 + 16)
                pe.wait_ge(probs_ready, b * NC)
                pe.wait_ge(wo_ready, 1)
                for h in range(HALVES):
                    for c in range(KT):
                        last = nc.tensor.matmul(qkv_ps[0:3 * DK, BANK * h:BANK * (h + 1)], w_qkv[:, c, :],
                                                xb[:, c, BANK * h:BANK * (h + 1)],
                                                start=(c == 0), stop=(c == KT - 1))
                last.then_inc(qkv_done, 1)
                pe.wait_ge(v_copied, b + 1)
                pe.wait_ge(turned_copied[0], b * NC)
                pe.wait_ge(q_ready, b + 1)
                pe.wait_ge(k_ready, b + 1)
                pe.wait_ge(mask_row_ready, b + 1)
                scores(b, 0)
                for c in range(NC):
                    last = nc.tensor.transpose(turn_ps[0][:, DK * c:DK * (c + 1)],
                                               v_t[:, P * c:P * (c + 1)],
                                               ident[VROW:VROW + DK, VROW:VROW + DK])
                last.then_inc(v_turned, 1)
                for t in range(1, NC):
                    scores(b, t)
                    turn(b, t - 1)
                    if t == TILES:
                        head(b, 0)
                    if t > TILES:
                        output(b, t - TILES - 1)
                output(b, TILES - 1)
                turn(b, NC - 1)
                head(b, 1)
                for t in range(TILES, NC):
                    output(b, t)

            with pe.Fori(1, 1 + STAGES * STEPS, STAGES) as first:
                for s in range(STAGES):
                    now = pe.snap(first + s) if s else first
                    begun = [False] * NCH
                    seen = [False] * NCH
                    left = [NCH] * NCH
                    for kj, j in ORDER:
                        if not seen[kj]:
                            pe.wait_ge(parts_ready[kj], now)
                            seen[kj] = True
                        left[j] -= 1
                        n0, n1 = CHUNKS[j]
                        for n in range(n0, n1):
                            col = MOVING * (n - n0)
                            for k in range(*CHUNKS[kj]):
                                for part in range(PARTS):
                                    last = nc.tensor.matmul(
                                        ps[:, NCH * (s % 2) + j, col:col + MOVING],
                                        coup[:, k, part, P * n:P * (n + 1)],
                                        tanh_parts[:, s % 2, k, :],
                                        start=not begun[j],
                                        stop=(left[j] == 0 and k == CHUNKS[kj][1] - 1 and part == PARTS - 1),
                                        skip_group_check=True)
                                    begun[j] = True
                        if left[j] == 0:
                            last.then_inc(product_done[j], 1)

        @block.vector
        def _(dve):
            V = nc.vector

            def axpy(out, a, factor, c, op1=ALU.add):
                return V.scalar_tensor_tensor(out=out, in0=a, scalar=factor, in1=c, op0=ALU.mult, op1=op1)

            dve.wait_ge(pool_ready, 8)
            V.tensor_reduce(stack_sum[:, :], stack[:, :, :].rearrange("p i d -> p d i"), AX.X, ALU.add)\
             .then_inc(stack_ready, 1)
            dve.wait_ge(wo_summed, 1)
            V.tensor_copy(wo_sum[:, :], head_ps[0:DK, :]).then_inc(wo_ready, 1)
            dve.wait_ge(coup_loaded, 16 * NC)
            for c in range(NC):
                last = V.tensor_reduce(col_max[:, c:c + 1], coup_stage(c), AX.X, ALU.max,
                                       apply_absolute_value=True)
            last.then_inc(maxes_ready, 1)
            dve.wait_ge(maxes_ready, 1)
            V.tensor_reduce(all_max[:, :], col_max[:, :], AX.X, ALU.max).then_inc(maxes_ready, 1)
            dve.wait_ge(max_turned, 1)
            V.tensor_reduce(top[:, :], small_ps[0:1, 0:P], AX.X, ALU.max).then_inc(top_ready, 1)
            dve.wait_ge(max_spread, 1)
            V.tensor_scalar(all_max[:, :], small_ps[:, 0:1], 2.0 ** -100, 2.0 ** 100, ALU.max, ALU.min)\
             .then_inc(setup, 1)
            dve.wait_ge(setup, 1)
            V.tensor_scalar(power[:, :].bitcast(I32), all_max[:, :].bitcast(I32), 0x7f800000, None,
                            ALU.bitwise_and).then_inc(setup, 1)
            dve.wait_ge(setup, 2)
            V.reciprocal(inv_power[:, :], power[:, :]).then_inc(setup, 1)
            dve.wait_ge(setup, 3)
            V.tensor_scalar(coup_scale[:, :], inv_power[:, :], 2.0 ** COUP_EXP, None, ALU.mult)\
             .then_inc(scale_ready, 1)
            for s in range(STAGES):
                last = V.tensor_scalar(step_scale[:, s:s + 1], power[:, :], 2.0 ** -COUP_EXP,
                                       STEP[s] / TANH_SCALE, ALU.mult, ALU.mult)
            last.then_inc(setup, 1)
            dve.wait_ge(scale_ready, 1)
            for c in range(NC):
                dve.wait_ge(coup_high, c + 1)
                V.scalar_tensor_tensor(out=coup[:, c, 1, :], in0=coup_stage(c), scalar=coup_scale[:, 0:1],
                                       in1=coup[:, c, 0, :], op0=ALU.mult, op1=ALU.subtract)\
                 .then_inc(coup_low, 1)

            def row_max(b, t):
                dve.wait_ge(scores_done, b * NC + (t + 1))
                V.tensor_reduce(neg_max[:, t:t + 1], score_ps[t % 2], AX.X, ALU.max, negate=True)\
                 .then_inc(max_ready, 1)

            def copy_turned_low(b, t):
                dve.wait_ge(turned[0], b * NC + (t + 1))
                q0 = P * (t % TILES)
                if t % TILES == 0:
                    dve.wait_ge(head_done, b * HALVES + t // TILES)
                V.tensor_copy(probs_t[:, 0:4, q0:q0 + P], turn_ps[0].rearrange("p (k q) -> p k q", q=P))\
                 .then_inc(turned_copied[0], 1)

            def scale_rows(b, half):
                r = slice(TILES * half, TILES * (half + 1))
                dve.wait_ge(probs_ready, b * NC + TILES * (half + 1))
                V.reciprocal(inv_sum[:, r], row_sum[:, r]).then_inc(inv_ready, 1)
                dve.wait_ge(inv_ready, b * HALVES + (half + 1))
                V.tensor_tensor(row_scale[:, r].rearrange("p (c o) -> p c o", o=1),
                                inv_sum[:, r].rearrange("p (c o) -> p c o", o=1),
                                cond_sb[:, r, bass.ds(b, 1)], ALU.mult).then_inc(row_scale_ready, 1)

            def add_output(b, t):
                dve.wait_ge(out_done, b * NC + (t + 1))
                dve.wait_ge(row_scale_ready, b * HALVES + (t // TILES + 1))
                column = steps[:, :, bass.ds(b + B * t, 1)].rearrange("p t o -> p (t o)")
                axpy(column, out_ps[t % 2], row_scale[:, t:t + 1], column).then_inc(out_added, 1)

            dve.wait_ge(consts_loaded, 16 * 5)
            dve.wait_ge(drive_loaded, 16 * 8)
            with dve.Fori(0, B) as b:
                dve.wait_ge(qkv_done, b + 1)
                dve.wait_ge(mask_loaded, b * 16 + 16)
                axpy(k_aug[0:DK, :], qkv_ps[DK:2 * DK, :], DK ** -0.5, mask_bc[0:DK, :], ALU.mult)\
                    .then_inc(k_ready, 1)
                V.tensor_scalar(k_aug[DK:DK + 1, :], mask_bc[DK:DK + 1, :], -MASKED, MASKED, ALU.mult, ALU.add)\
                 .then_inc(mask_row_ready, 1)
                dve.wait_ge(v_turned, b + 1)
                V.tensor_copy(v_sb[:, :, :].rearrange("p c d -> p (c d)"), turn_ps[0][:, 0:NC * DK])\
                 .then_inc(v_ready, 1)
                for t in range(NC):
                    row_max(b, t)
                    if t >= 1:
                        copy_turned_low(b, t - 1)
                    if t == TILES:
                        scale_rows(b, 0)
                    if t > TILES:
                        add_output(b, t - TILES - 1)
                add_output(b, TILES - 1)
                copy_turned_low(b, NC - 1)
                scale_rows(b, 1)
                for t in range(TILES, NC):
                    add_output(b, t)

            V.memset(tanh_parts[:, :, :, :], 0.0)
            V.tensor_copy(q_st[0][:, :], cond_sb[:, :, :].rearrange("p c b -> p (c b)"))
            V.tensor_scalar(p_st[:, :], cond_sb[:, :, :].rearrange("p c b -> p (c b)"), -SHIFT, None, ALU.add)
            V.memset(z[:, :], 0.0).then_inc(setup, 1)
            dve.wait_ge(setup, 5)
            for c in range(NC):
                last = V.tensor_scalar(cols(bias_b, (c, c + 1)), cols(z, (c, c + 1)), bias_sb[:, c:c + 1],
                                       -SHIFT, ALU.add, ALU.add)
            last.then_inc(setup, 1)
            dve.wait_ge(setup, 6)
            for j in range(NCH):
                V.engine_nop().then_inc(q_next[j], 1)
            V.tensor_tensor(drive_b[:, :], steps[:, 0, :], bias_b[:, :], ALU.add).then_inc(setup, 1)
            dve.wait_ge(setup, 7)
            V.tensor_tensor(drive_p[:, :], drive_b[:, :], p_st[:, :], ALU.subtract)\
             .then_inc(drive_p_ready, STAGES)


            def add_high(s, j, now):
                if j == 0:
                    dve.wait_ge(base_ready, now)
                dve.wait_ge(product_done[j], now)
                axpy(by_block(half_sum, CHUNKS[j]), product(s, j, 0), step_scale[:, s:s + 1],
                     by_block(base, CHUNKS[j])).then_inc(half_ready[j], 1)

            def add_low(s, j, now):
                dve.wait_ge(half_ready[j], now)
                out = q_st[s + 1] if s + 1 < STAGES else q_raw
                axpy(by_block(out, CHUNKS[j]), product(s, j, 1), step_scale[:, s:s + 1],
                     by_block(half_sum, CHUNKS[j])).then_inc(q_next[j], 1)

            def split_low(parity, j, made):
                dve.wait_ge(high_ready[j], made)
                axpy(tanh_part(parity, j, 1), by_block(tanh_sb, CHUNKS[j]), TANH_SCALE,
                     tanh_part(parity, j, 0), ALU.subtract).then_inc(parts_ready[j], 1)

            def cubic_of(stage, count):
                dve.wait_ge(square_ready if stage else square0_ready, count)
                V.scalar_tensor_tensor(out=cubic[:, :], in0=(square if stage else square0)[:, :], scalar=-3.0,
                                       in1=q_st[stage][:, :], op0=ALU.add, op1=ALU.mult)\
                 .then_inc(cubic_ready, 1)

            def base_of(stage, made):
                dve.wait_ge(cubic_ready, made)
                axpy(base[:, :], cubic[:, :], -STEP[stage] / 3, [z, z2, z3, z][stage][:, :])\
                    .then_inc(base_ready, 1)

            def z_of_first():
                axpy(z[:, :], drive_p[:, :], DT / 2, q_st[0][:, :])

            def z_of_second():
                axpy(z2[:, :], g0[:, :], -DT / 2 * RISE, z[:, :])

            def y_of():
                axpy(y[:, :], drive_p[:, :], DT, q_st[0][:, :])

            def y_less_g0():
                axpy(y_less[:, :], g0[:, :], -DT * RISE * G1[0], y[:, :])

            def z_of_third():
                axpy(z3[:, :], rise[0][:, :], -DT * RISE * G1[1], y_less[:, :])

            def rise_of(stage):
                V.tensor_tensor(rise[stage - 1][:, :], q_st[stage][:, :], q_st[0][:, :], ALU.subtract)

            def q_sum_g0():
                axpy(q_sum[0][:, :], g0[:, :], Q_SUM[0] / (DT / 2), drive_p[:, :])

            def q_sum_r1():
                axpy(q_sum[1][:, :], q_sum[0][:, :], DT / 2 / Q_SUM[1], rise[0][:, :])

            def q_sum_r2():
                axpy(q_sum[2][:, :], rise[1][:, :], Q_SUM[2] / Q_SUM[1], q_sum[1][:, :])

            def z_without_last(now):
                dve.wait_ge(q_share_ready, now)
                axpy(z_rest[:, :], q_sum[2][:, :], THIRD * Q_SUM[1], q_share[:, :])

            def z_of_last(made):
                dve.wait_ge(q_next[NCH - 1], made)
                axpy(z[:, :], q_st[3][:, :], THIRD, z_rest[:, :])

            def g0_of():
                axpy(g0[:, :], p_st[:, :], -BETA, q_st[0][:, :])

            def p_sum_g0():
                axpy(p_sum[0][:, :], g0[:, :], P_SUM[0], q_st[0][:, :], ALU.subtract)

            def p_sum_r(k):
                axpy(p_sum[k][:, :], rise[k - 1][:, :], P_SUM[k], p_sum[k - 1][:, :])

            def p_sum_q3():
                V.tensor_tensor(p_sum[3][:, :], p_sum[2][:, :], q_st[3][:, :], ALU.add)

            def p_next():
                axpy(p_raw[:, :], p_sum[3][:, :], DT / 6 * EPS, p_st[:, :])

            def clip_p():
                V.tensor_scalar(p_st[:, :], p_raw[:, :], -CLAMP - SHIFT, CLAMP - SHIFT, ALU.max, ALU.min)\
                 .then_inc(p_ready, STAGES)

            def look_ahead(at):
                V.tensor_tensor(drive_b[:, :], drive_cols[:, bass.ds(at, COLS)], bias_b[:, :], ALU.add)

            def drive_less_p(now):
                dve.wait_ge(p_ready, now)
                V.tensor_tensor(drive_p[:, :], drive_b[:, :], p_st[:, :], ALU.subtract)

            def clip_q(made):
                dve.wait_ge(q_next[NCH - 1], made)
                V.tensor_scalar(q_st[0][:, :], q_raw[:, :], -CLAMP, CLAMP, ALU.max, ALU.min)\
                 .then_inc(clipped, 1)

            def square_of_clipped(steps_done):
                dve.wait_ge(clipped, steps_done)
                V.tensor_tensor(square0[:, :], q_st[0][:, :], q_st[0][:, :], ALU.mult)\
                 .then_inc(square0_ready, 1)

            def trace(at):
                at = drive_cols[:, bass.ds(at, COLS)]
                V.tensor_tensor(at, at, q_st[0][:, :], ALU.add).then_inc(traced, 1)

            dve.wait_ge(drive_p_ready, STAGES)
            z_of_first()
            V.tensor_tensor(square0[:, :], q_st[0][:, :], q_st[0][:, :], ALU.mult).then_inc(setup, 1)
            for j in range(NCH):
                split_low(0, j, 1)
            dve.wait_ge(setup, 8)
            V.scalar_tensor_tensor(out=cubic[:, :], in0=square0[:, :], scalar=-3.0, in1=q_st[0][:, :],
                                   op0=ALU.add, op1=ALU.mult).then_inc(cubic_ready, 1)
            base_of(0, 1)

            def stage(s, now):
                parity = (s + 1) % 2
                if s == 2:
                    rise_of(2)
                if s == 3:
                    p_sum_q3()
                add_high(s, 0, now)
                add_high(s, 1, now)
                add_low(s, 0, now)
                add_low(s, 1, now)
                if s == 0:
                    g0_of()
                    y_of()
                if s == 1:
                    rise_of(1)
                    p_sum_g0()
                if s == 2:
                    q_sum_r2()
                    p_sum_r(2)
                if s == 3:
                    p_next()
                    look_ahead((now + STAGES) * (COLS // STAGES))
                made = after(now)
                add_high(s, 2, now)
                split_low(parity, 0, made)
                split_low(parity, 1, made)
                add_low(s, 2, now)
                add_high(s, 3, now)
                if s == 0:
                    z_of_second()
                if s == 1:
                    z_of_third()
                if s == 2:
                    z_without_last(now)
                if s == 3:
                    clip_p()
                    steps_done = steps_until(now)
                add_low(s, 3, now)
                if s == 0:
                    y_less_g0()
                if s == 1:
                    q_sum_r1()
                if s == 2:
                    trace((now - 3) * (COLS // STAGES))
                if s == 3:
                    drive_less_p(now)
                    clip_q(made)
                split_low(parity, 2, made)
                if s == 0:
                    q_sum_g0()
                if s == 1:
                    p_sum_r(1)
                if s == 2:
                    z_of_last(made)
                if s == 3:
                    square_of_clipped(steps_done)
                    z_of_first()
                    split_low(parity, 3, made)
                    cubic_of(0, steps_done)
                else:
                    cubic_of(s + 1, made)
                    split_low(parity, 3, made)
                base_of((s + 1) % STAGES, made)
                return made

            def after(now):
                return now + 1 if isinstance(now, int) else dve.snap(now + 1)

            def steps_until(now):
                return now // STAGES if isinstance(now, int) else dve.snap(now >> 2)

            order = [(s + 1) % STAGES for s in range(STAGES)] * UNROLLED
            stage(0, 1)
            with dve.Fori(2, 2 + STAGES * (STEPS - UNROLLED), STAGES * UNROLLED) as now:
                for s in order:
                    now = stage(s, now)
            now = 2 + STAGES * (STEPS - UNROLLED)
            for s in order[:-1]:
                now = stage(s, now)
            trace(STEPS * COLS)


def kernel(x, cond_2048, L0_cond_Wq, L0_cond_Wk, L0_cond_Wv, L0_cond_Wo, L1_cond_coupling, L1_cond_bias):
    import numpy as np
    import concourse.bacc as bacc
    from concourse.bass_utils import run_bass_kernel_spmd

    x, cond, coupling, bias = (np.asarray(a) for a in (x, cond_2048, L1_cond_coupling, L1_cond_bias))
    arrays = {
        "x": x,
        "x_pt": x.reshape(B, T, NC, P).transpose(3, 1, 2, 0).reshape(P, T, COLS),
        "cond": cond,
        "cond_p": cond.reshape(B, NC, P).transpose(2, 1, 0),
        "wq": np.asarray(L0_cond_Wq)[1],
        "wk": np.asarray(L0_cond_Wk)[1],
        "wv": np.asarray(L0_cond_Wv)[1],
        "wo": np.asarray(L0_cond_Wo),
        "coupling_t": coupling.T,
        "bias_p": bias.reshape(NC, P).T,
    }
    arrays = {k: np.ascontiguousarray(a) for k, a in arrays.items()}
    nc = bacc.Bacc("TRN2", target_bir_lowering=False, num_devices=1,
                   dynamic_dma_scratch_size=1024)
    args = [nc.dram_tensor(f"in_{k}", a.shape, mybir.dt.from_np(a.dtype), kind="ExternalInput").ap()
            for k, a in arrays.items()]
    out = nc.dram_tensor("out_pt", (P, T, COLS), F32, kind="ExternalOutput").ap()
    build(nc, *args, out)
    r = run_bass_kernel_spmd(nc, [{f"in_{k}": a for k, a in arrays.items()}], core_ids=[0])
    got = np.asarray(r.results[0]["out_pt"])
    return np.ascontiguousarray(got.reshape(P, T, NC, B).transpose(3, 1, 2, 0).reshape(B, T, N))
```

```python
import concourse.bass as bass
from concourse import mybir
from contextlib import ExitStack

F32 = mybir.dt.float32
F16 = mybir.dt.float16
I32 = mybir.dt.int32
ALU = mybir.AluOpType
ACT = mybir.ActivationFunctionType
AX = mybir.AxisListType

P = 128
B = 8
T = 512
N = 1024
NC = N // P
KT = T // P
DK = 32
VROW = 2 * DK
COLS = NC * B
BANK = 512
NBANK = 8
HALVES = N // BANK
TILES = BANK // P
MASKED = -1e30

DT, EPS, ALPHA, BETA, CLAMP = 0.01, 0.08, 0.7, 0.8, 20.0
SHIFT = ALPHA / BETA
STAGES = 4
STEPS = T
RISE = DT / 2 * EPS
STEP = [DT / 2, DT / 2, DT, DT / 6]
THIRD = 5592405 / 2 ** 24

G1 = [1 - BETA * RISE, 1.0, 0.0]
G2 = [1 - BETA * RISE * G1[0], -BETA * RISE * G1[1], 1.0]
G3 = [1 - 2 * BETA * RISE * G2[0], -2 * BETA * RISE * G2[1], -2 * BETA * RISE * G2[2]]
P_SUM = [(k == 0) + 2 * G1[k] + 2 * G2[k] + G3[k] for k in range(3)]
Q_SUM = [-DT * RISE * G2[0], 1 - DT * RISE * G2[1], 2 - DT * RISE * G2[2]]

CHUNKS = [(0, 1), (1, 3), (3, 6), (6, 8)]
NCH = len(CHUNKS)
ORDER = [(0, 2), (0, 0), (0, 1), (1, 2), (1, 3), (1, 0), (1, 1), (2, 0), (2, 1), (3, 0), (3, 1), (3, 2),
         (2, 2), (0, 3), (3, 3), (2, 3)]
PARTS = 2
MOVING = 32
PE_STAGES = 2
UNROLLED = 2
TANH_SCALE = 4096.0
COUP_EXP = 14
DRIVE_LOADS = 8
MATRICES = 4
FILLED = MATRICES + 8
STORE_STEPS = 32


def build(nc, x, x_pt, cond, cond_p, wq, wk, wv, wo, coupling_t, bias_p, out_pt):
    ctx = ExitStack()
    with ctx:
        def sb(name, shape, dt=F32):
            return ctx.enter_context(nc.sbuf_tensor(name, shape, dt))

        def sem(name):
            return ctx.enter_context(nc.semaphore(name))

        drive = sb("drive", [P, T + 2, COLS])
        steps = drive[:, 1:1 + T, :]
        drive_cols = drive[:, :, :].rearrange("p t c -> p (t c)")
        coup = sb("coup", [P, NC, PARTS, N], F16)
        tanh_parts = sb("tanh_parts", [P, 2, NC, MOVING], F16)

        xb = sb("xb", [P, KT, N])
        w_qkv = sb("w_qkv", [P, KT, 3 * DK])
        q_aug = sb("q_aug", [P, N])
        k_aug = sb("k_aug", [P, N])
        head_t = sb("head_t", [P, BANK])
        wo_sum = sb("wo_sum", [P, T])
        mask_v = sb("mask_v", [P, N])
        mask_bc = mask_v[0:DK + 1, :]
        v_t = mask_v[VROW:VROW + DK, :]
        v_sb = sb("v_sb", [P, NC, DK])
        probs = sb("probs", [P, 2, N])
        probs_t = sb("probs_t", [P, NC, BANK])
        neg_max = sb("neg_max", [P, NC])
        row_sum = sb("row_sum", [P, NC])
        inv_sum = sb("inv_sum", [P, NC])
        row_scale = sb("row_scale", [P, NC])
        ident = sb("ident", [P, P])
        stack = sb("stack", [P, P // DK, DK])
        stack_sum = sb("stack_sum", [P, DK])
        ones_row = sb("ones_row", [1, P])

        col_max = sb("col_max", [P, NC])
        all_max = sb("all_max", [P, 1])
        top = sb("top", [1, 1])
        power = sb("power", [P, 1])
        inv_power = sb("inv_power", [P, 1])
        coup_scale = sb("coup_scale", [P, 1])

        cond_sb = sb("cond_sb", [P, NC, B])
        bias_sb = sb("bias_sb", [P, NC])
        step_scale = sb("step_scale", [P, STAGES])
        states = iter(range(0, KT * N, COLS))

        def state():
            first = next(states)
            return xb[:, :, :].rearrange("p c n -> p (c n)")[:, first:first + COLS]

        q_st = [state() for s in range(STAGES)]
        q_raw = state()
        half_sum = state()
        tanh_sb = state()
        square = state()
        square0 = state()
        cubic = state()
        base = state()
        z = state()
        z2 = state()
        z3 = state()
        p_st = state()
        p_raw = state()
        bias_b = state()
        drive_b = state()
        drive_p = state()
        g0 = state()
        y = state()
        y_less = state()
        q_share = state()
        rise = [state() for k in (1, 2)]
        q_sum = [state() for k in range(3)]
        p_sum = [state() for k in range(4)]
        z_rest = state()

        ps = ctx.enter_context(nc.psum_tensor("ps", [P, NBANK, BANK], F32))
        score_ps = [ps[:, 0:2, :].rearrange("p a n -> p (a n)"), ps[:, 2:4, :].rearrange("p a n -> p (a n)")]
        turn_ps = [ps[:, 4, :], ps[:, 5, :]]
        head_ps = ps[:, 6, :]
        out_ps = [ps[:, 7, :], ps[:, 6, :]]
        qkv_ps = score_ps[0]
        small_ps = ps[:, 7, :]

        coup_loaded = [sem(f"coup_loaded{c}") for c in range(NC)]
        consts_loaded = sem("consts_loaded")
        wo_loaded = sem("wo_loaded")
        drive_loaded = sem("drive_loaded")
        x_loaded = sem("x_loaded")
        mask_loaded = sem("mask_loaded")
        stored = sem("stored")

        pool_ready = sem("pool_ready")
        stack_ready = sem("stack_ready")
        wo_summed = sem("wo_summed")
        wo_ready = sem("wo_ready")
        maxes_ready = sem("maxes_ready")
        max_turned = sem("max_turned")
        top_ready = sem("top_ready")
        max_spread = sem("max_spread")
        scale_ready = sem("scale_ready")
        coup_high = sem("coup_high")
        coup_low = sem("coup_low")
        setup = sem("setup")

        qkv_done = sem("qkv_done")
        q_ready = sem("q_ready")
        k_ready = sem("k_ready")
        v_copied = sem("v_copied")
        mask_row_ready = sem("mask_row_ready")
        v_turned = sem("v_turned")
        v_ready = sem("v_ready")
        scores_done = sem("scores_done")
        max_ready = sem("max_ready")
        probs_ready = sem("probs_ready")
        turned = [sem("turned0"), sem("turned1")]
        turned_copied = [sem("turned_copied0"), sem("turned_copied1")]
        head_done = sem("head_done")
        head_ready = sem("head_ready")
        inv_ready = sem("inv_ready")
        row_scale_ready = sem("row_scale_ready")
        out_done = sem("out_done")
        out_added = sem("out_added")

        product_done = [sem(f"product_done{j}") for j in range(NCH)]
        half_ready = [sem(f"half_ready{j}") for j in range(NCH)]
        q_next = [sem(f"q_next{j}") for j in range(NCH)]
        tanh_ready = [sem(f"tanh_ready{j}") for j in range(NCH)]
        high_ready = [sem(f"high_ready{j}") for j in range(NCH)]
        parts_ready = [sem(f"parts_ready{j}") for j in range(NCH)]
        square_ready = sem("square_ready")
        cubic_ready = sem("cubic_ready")
        base_ready = sem("base_ready")
        p_ready = sem("p_ready")
        q_share_ready = sem("q_share_ready")
        clipped = sem("clipped")
        square0_ready = sem("square0_ready")
        traced = sem("traced")
        drive_p_ready = sem("drive_p_ready")

        def cols(t, blocks):
            return t[:, B * blocks[0]:B * blocks[1]]

        def by_block(t, blocks):
            return cols(t, blocks).rearrange("p (c b) -> p c b", b=B)

        def product(stage, j, part):
            w = CHUNKS[j][1] - CHUNKS[j][0]
            return ps[:, NCH * (stage % 2) + j, 0:w * MOVING].rearrange(
                "p (c m) -> p c m", m=MOVING)[:, :, B * part:B * (part + 1)]

        def tanh_part(parity, j, part):
            return tanh_parts[:, parity, CHUNKS[j][0]:CHUNKS[j][1], B * part:B * (part + 1)]

        def coup_stage(c):
            first = T - (NC - c) * N // COLS
            return steps[:, first:first + N // COLS, :].rearrange("p t c -> p (t c)")

        def wait_if_any(engine, semaphore, count):
            if not (isinstance(count, int) and count == 0):
                engine.wait_ge(semaphore, count)

        block = ctx.enter_context(nc.Block())

        @block.sync
        def _(sp):
            for i, w in enumerate((wq, wk, wv)):
                sp.dma_start(w_qkv[:, :, DK * i:DK * (i + 1)],
                             w.rearrange("(c p) d -> p c d", p=P)).then_inc(consts_loaded, 16)
            sp.dma_start(cond_sb[:, :, :], cond_p).then_inc(consts_loaded, 16)
            sp.dma_start(bias_sb[:, :], bias_p).then_inc(consts_loaded, 16)

            def load(b):
                wait_if_any(sp, qkv_done, b)
                sp.dma_start(xb[:, :, :], x[bass.ds(b, 1), :, :].rearrange("o (c p) n -> p (o c) n", p=P))\
                  .then_inc(x_loaded, 16)
                wait_if_any(sp, k_ready, b)
                wait_if_any(sp, mask_row_ready, b)
                sp.dma_start(mask_bc[:, :], cond[bass.ds(b, 1), :].broadcast_to([DK + 1, N]))\
                  .then_inc(mask_loaded, 16)

            load(0)
            for c in range(NC):
                sp.dma_start(coup_stage(c), coupling_t[P * c:P * (c + 1), :]).then_inc(coup_loaded[c], 16)
            for i in range(DRIVE_LOADS):
                if i == DRIVE_LOADS - DRIVE_LOADS // 4:
                    sp.wait_ge(coup_high, NC)
                    sp.wait_ge(coup_low, NC)
                s = slice(i * T // DRIVE_LOADS, (i + 1) * T // DRIVE_LOADS)
                sp.dma_start(steps[:, s, :], x_pt[:, s, :]).then_inc(drive_loaded, 16)
            with sp.Fori(1, B) as b:
                load(b)
            with sp.Fori(0, T // STORE_STEPS) as i:
                sp.wait_ge(traced, i * STORE_STEPS + (1 + STORE_STEPS))
                sp.dma_start(out_pt[:, bass.ds(i * STORE_STEPS, STORE_STEPS), :],
                             steps[:, bass.ds(i * STORE_STEPS, STORE_STEPS), :]).then_inc(stored, 16)
            sp.wait_ge(stored, 16 * (T // STORE_STEPS))

        @block.gpsimd
        def _(pool):
            nc.gpsimd.memset(ident[:, :], 0.0).then_inc(pool_ready, 1)
            pool.wait_ge(pool_ready, 1)
            nc.gpsimd.memset(stack[:, :, :], 0.0).then_inc(pool_ready, 1)
            pool.wait_ge(pool_ready, 2)
            nc.gpsimd.affine_select(out=ident[:, :], in_=ident[:, :], compare_op=ALU.not_equal, fill=1.0,
                                    base=0, pattern=[[-1, P]], channel_multiplier=1).then_inc(pool_ready, 1)
            pool.wait_ge(pool_ready, 3)
            nc.gpsimd.affine_select(out=stack[:, :, :], in_=stack[:, :, :], compare_op=ALU.not_equal,
                                    fill=1.0, base=0, pattern=[[-DK, P // DK], [-1, DK]],
                                    channel_multiplier=1).then_inc(pool_ready, 1)
            fills = [(wo_sum[:, :], 0.0), (ones_row[:, :], 1.0), (head_t[:, :], 0.0),
                     (q_aug[:, :], 0.0), (k_aug[:, :], 0.0), (q_aug[DK:DK + 1, :], 1.0),
                     (drive[:, 0, :], 0.0), (drive[:, 1 + T, :], 0.0)]
            for i, (buffer, value) in enumerate(fills):
                pool.wait_ge(pool_ready, 4 + i)
                nc.gpsimd.memset(buffer, value).then_inc(pool_ready, 1)

        @block.scalar
        def _(act):
            act.dma_start(probs[:, :, :].rearrange("p a (c n) -> p (a c) n", n=T),
                          wo.rearrange("(c p) n -> p c n", p=P)).then_inc(wo_loaded, 16)

            def copy_turned(b, t):
                act.wait_ge(turned[1], b * NC + (t + 1))
                q0 = P * (t % TILES)
                if t % TILES == 0:
                    wait_if_any(act, head_done, b * HALVES + t // TILES)
                nc.scalar.activation(probs_t[:, 4:8, q0:q0 + P],
                                     turn_ps[1].rearrange("p (k q) -> p k q", q=P), ACT.Copy)\
                  .then_inc(turned_copied[1], 1)

            def copy_q_v(b):
                act.wait_ge(qkv_done, b + 1)
                nc.scalar.activation(q_aug[0:DK, :], qkv_ps[0:DK, :], ACT.Copy).then_inc(q_ready, 1)
                nc.scalar.activation(v_t[:, :], qkv_ps[2 * DK:3 * DK, :], ACT.Copy).then_inc(v_copied, 1)

            def copy_head(b, half):
                act.wait_ge(head_done, b * HALVES + (half + 1))
                wait_if_any(act, out_done, b * NC + TILES * half)
                nc.scalar.activation(head_t[0:DK, :], head_ps[0:DK, :], ACT.Copy).then_inc(head_ready, 1)

            def attend(b, more):
                for t in range(NC):
                    act.wait_ge(max_ready, b * NC + (t + 1))
                    if t < 2:
                        wait_if_any(act, turned[1], b * NC)
                    else:
                        act.wait_ge(turned[1], b * NC + (t - 1))
                    nc.scalar.activation(probs[:, t % 2, :], score_ps[t % 2], ACT.Exp,
                                         bias=neg_max[:, t:t + 1],
                                         accum_out=row_sum[:, t:t + 1]).then_inc(probs_ready, 1)
                    if t == TILES + 1:
                        copy_head(b, 0)
                    if t >= 1:
                        copy_turned(b, t - 1)
                if more:
                    copy_q_v(b + 1)
                copy_turned(b, NC - 1)
                copy_head(b, 1)

            act.wait_ge(pool_ready, FILLED)
            copy_q_v(0)
            act.wait_ge(scale_ready, 1)
            for c in range(NC):
                nc.scalar.activation(coup[:, c, 0, :], coup_stage(c), ACT.Copy,
                                     scale=coup_scale[:, 0:1]).then_inc(coup_high, 1)
            attend(0, True)
            with act.Fori(1, B - 1) as b:
                attend(b, True)
            attend(B - 1, False)

            def tanh(q, j, count):
                act.wait_ge(q_next[j], count)
                nc.scalar.activation(cols(tanh_sb, CHUNKS[j]), cols(q, CHUNKS[j]), ACT.Tanh)\
                  .then_inc(tanh_ready[j], 1)

            def split_high(parity, j, count):
                act.wait_ge(tanh_ready[j], count)
                nc.scalar.activation(tanh_part(parity, j, 0), by_block(tanh_sb, CHUNKS[j]), ACT.Copy,
                                     scale=TANH_SCALE).then_inc(high_ready[j], 1)

            for j in range(NCH):
                tanh(q_st[0], j, 1)
                split_high(0, j, 1)

            with act.Fori(1, 1 + STAGES * STEPS, STAGES * UNROLLED) as now:
                for u in range(STAGES * UNROLLED):
                    s, parity = u % STAGES, (u + 1) % 2
                    made = act.snap(now + 1)
                    q = q_st[s + 1] if s + 1 < STAGES else q_raw
                    tanh(q, 0, made)
                    tanh(q, 1, made)
                    split_high(parity, 0, made)
                    split_high(parity, 1, made)
                    tanh(q, 2, made)
                    split_high(parity, 2, made)
                    tanh(q, 3, made)
                    if s + 1 < STAGES:
                        nc.scalar.activation(square[:, :], q_st[s + 1][:, :], ACT.Square)\
                          .then_inc(square_ready, 2 if s == 0 else 1)
                    split_high(parity, 3, made)
                    if s == 0:
                        nc.scalar.activation(q_share[:, :], q_st[0][:, :], ACT.Copy, scale=1 - THIRD)\
                          .then_inc(q_share_ready, STAGES)
                    now = made

        @block.tensor
        def _(pe):
            pe.wait_ge(stack_ready, 1)
            pe.wait_ge(wo_loaded, 16)
            wo_rows = probs[:, :, :].rearrange("p a (c n) -> p (a c) n", n=T)
            for c in range(KT):
                last = nc.tensor.matmul(head_ps[0:DK, :], stack_sum[:, :], wo_rows[:, c, :],
                                        start=(c == 0), stop=(c == KT - 1))
            last.then_inc(wo_summed, 1)
            def scores(b, t):
                if t == 1:
                    wait_if_any(pe, probs_ready, b * NC)
                if t >= 2:
                    pe.wait_ge(probs_ready, b * NC + (t - 1))
                for h in range(HALVES):
                    last = nc.tensor.matmul(score_ps[t % 2][:, BANK * h:BANK * (h + 1)],
                                            q_aug[:, P * t:P * (t + 1)], k_aug[:, BANK * h:BANK * (h + 1)],
                                            start=True, stop=True)
                last.then_inc(scores_done, 1)

            def turn(b, t):
                pe.wait_ge(probs_ready, b * NC + (t + 1))
                for h in range(2):
                    if t == 0 and h == 0:
                        pe.wait_ge(v_ready, b + 1)
                    elif t == 0:
                        wait_if_any(pe, turned_copied[h], b * NC)
                    else:
                        pe.wait_ge(turned_copied[h], b * NC + t)
                    for k in range(4):
                        kb = 4 * h + k
                        last = nc.tensor.transpose(turn_ps[h][:, P * k:P * (k + 1)],
                                                   probs[:, t % 2, P * kb:P * (kb + 1)], ident[:, :])
                    last.then_inc(turned[h], 1)

            def head(b, half):
                for h in range(2):
                    pe.wait_ge(turned_copied[h], b * NC + TILES * (half + 1))
                if half == 0:
                    wait_if_any(pe, out_added, b * NC)
                else:
                    pe.wait_ge(out_added, b * NC + TILES)
                for k in range(NC):
                    last = nc.tensor.matmul(head_ps[0:DK, :], v_sb[:, k, :], probs_t[:, k, :],
                                            start=(k == 0), stop=(k == NC - 1))
                last.then_inc(head_done, 1)

            def output(b, t):
                pe.wait_ge(head_ready, b * HALVES + (t // TILES + 1))
                if t % TILES >= 2:
                    pe.wait_ge(out_added, b * NC + (t - 1))
                q0 = P * (t % TILES)
                nc.tensor.matmul(out_ps[t % 2], head_t[:, q0:q0 + P], wo_sum[:, :], start=True, stop=True)\
                  .then_inc(out_done, 1)

            def project(b):
                pe.wait_ge(x_loaded, b * 16 + 16)
                if not isinstance(b, int) or b > 0:
                    pe.wait_ge(probs_ready, b * NC - 1)
                for h in range(HALVES):
                    for c in range(KT):
                        last = nc.tensor.matmul(qkv_ps[0:3 * DK, BANK * h:BANK * (h + 1)], w_qkv[:, c, :],
                                                xb[:, c, BANK * h:BANK * (h + 1)],
                                                start=(c == 0), stop=(c == KT - 1))
                last.then_inc(qkv_done, 1)

            def attend(b, more):
                pe.wait_ge(v_copied, b + 1)
                wait_if_any(pe, turned_copied[0], b * NC)
                pe.wait_ge(q_ready, b + 1)
                pe.wait_ge(k_ready, b + 1)
                pe.wait_ge(mask_row_ready, b + 1)
                scores(b, 0)
                for c in range(NC):
                    last = nc.tensor.transpose(turn_ps[0][:, DK * c:DK * (c + 1)],
                                               v_t[:, P * c:P * (c + 1)],
                                               ident[VROW:VROW + DK, VROW:VROW + DK])
                last.then_inc(v_turned, 1)
                for t in range(1, NC):
                    scores(b, t)
                    if t == TILES + 1:
                        head(b, 0)
                    turn(b, t - 1)
                    if t > TILES + 1:
                        output(b, t - TILES - 2)
                if more:
                    project(b + 1)
                turn(b, NC - 1)
                for t in range(2, TILES):
                    output(b, t)
                head(b, 1)
                for t in range(TILES, NC):
                    output(b, t)

            pe.wait_ge(consts_loaded, 16 * 5)
            project(0)
            pe.wait_ge(maxes_ready, 2)
            pe.wait_ge(pool_ready, FILLED)
            nc.tensor.transpose(small_ps[0:1, 0:P], all_max[:, :], ident[:, :]).then_inc(max_turned, 1)
            pe.wait_ge(top_ready, 1)
            nc.tensor.matmul(small_ps[:, 0:1], ones_row[:, :], top[:, :], start=True, stop=True)\
              .then_inc(max_spread, 1)
            pe.wait_ge(wo_ready, 1)
            attend(0, True)
            with pe.Fori(1, B - 1) as b:
                attend(b, True)
            attend(B - 1, False)

            with pe.Fori(1, 1 + STAGES * STEPS, PE_STAGES) as now:
                for s in range(PE_STAGES):
                    begun = [False] * NCH
                    seen = [False] * NCH
                    left = [NCH] * NCH
                    for place, (kj, j) in enumerate(ORDER):
                        if not seen[kj]:
                            pe.wait_ge(parts_ready[kj], now)
                            seen[kj] = True
                        left[j] -= 1
                        n0, n1 = CHUNKS[j]
                        for n in range(n0, n1):
                            col = MOVING * (n - n0)
                            for k in range(*CHUNKS[kj]):
                                for part in range(PARTS):
                                    last = nc.tensor.matmul(
                                        ps[:, NCH * (s % 2) + j, col:col + MOVING],
                                        coup[:, k, part, P * n:P * (n + 1)],
                                        tanh_parts[:, s % 2, k, :],
                                        start=not begun[j],
                                        stop=(left[j] == 0 and k == CHUNKS[kj][1] - 1 and part == PARTS - 1),
                                        skip_group_check=True)
                                    begun[j] = True
                        if left[j] == 0:
                            last.then_inc(product_done[j], 1)
                        if place == len(ORDER) // 2:
                            after = pe.snap(now + 1)
                    now = after

        @block.vector
        def _(dve):
            V = nc.vector

            def axpy(out, a, factor, c, op1=ALU.add):
                return V.scalar_tensor_tensor(out=out, in0=a, scalar=factor, in1=c, op0=ALU.mult, op1=op1)

            dve.wait_ge(pool_ready, MATRICES)
            V.tensor_reduce(stack_sum[:, :], stack[:, :, :].rearrange("p i d -> p d i"), AX.X, ALU.add)\
             .then_inc(stack_ready, 1)
            dve.wait_ge(wo_summed, 1)
            dve.wait_ge(pool_ready, MATRICES + 1)
            V.tensor_copy(wo_sum[0:DK, :], head_ps[0:DK, :]).then_inc(wo_ready, 1)

            def row_max(b, t):
                dve.wait_ge(scores_done, b * NC + (t + 1))
                V.tensor_reduce(neg_max[:, t:t + 1], score_ps[t % 2], AX.X, ALU.max, negate=True)\
                 .then_inc(max_ready, 1)

            def copy_turned_low(b, t):
                dve.wait_ge(turned[0], b * NC + (t + 1))
                q0 = P * (t % TILES)
                if t % TILES == 0:
                    wait_if_any(dve, head_done, b * HALVES + t // TILES)
                V.tensor_copy(probs_t[:, 0:4, q0:q0 + P], turn_ps[0].rearrange("p (k q) -> p k q", q=P))\
                 .then_inc(turned_copied[0], 1)

            def scale_rows(b, half):
                r = slice(TILES * half, TILES * (half + 1))
                dve.wait_ge(probs_ready, b * NC + TILES * (half + 1))
                V.reciprocal(inv_sum[:, r], row_sum[:, r]).then_inc(inv_ready, 1)
                dve.wait_ge(inv_ready, b * HALVES + (half + 1))
                V.tensor_tensor(row_scale[:, r].rearrange("p (c o) -> p c o", o=1),
                                inv_sum[:, r].rearrange("p (c o) -> p c o", o=1),
                                cond_sb[:, r, bass.ds(b, 1)], ALU.mult).then_inc(row_scale_ready, 1)

            def add_output(b, t):
                dve.wait_ge(out_done, b * NC + (t + 1))
                dve.wait_ge(row_scale_ready, b * HALVES + (t // TILES + 1))
                column = steps[:, :, bass.ds(b + B * t, 1)].rearrange("p t o -> p (t o)")
                axpy(column, out_ps[t % 2], row_scale[:, t:t + 1], column).then_inc(out_added, 1)

            dve.wait_ge(consts_loaded, 16 * 5)

            dve.wait_ge(pool_ready, FILLED)

            def scale_k(b):
                dve.wait_ge(qkv_done, b + 1)
                dve.wait_ge(mask_loaded, b * 16 + 16)
                axpy(k_aug[0:DK, :], qkv_ps[DK:2 * DK, :], DK ** -0.5, mask_bc[0:DK, :], ALU.mult)\
                    .then_inc(k_ready, 1)
                V.tensor_scalar(k_aug[DK:DK + 1, :], mask_bc[DK:DK + 1, :], -MASKED, MASKED, ALU.mult, ALU.add)\
                 .then_inc(mask_row_ready, 1)

            def attend(b, more):
                dve.wait_ge(v_turned, b + 1)
                V.tensor_copy(v_sb[:, :, :].rearrange("p c d -> p (c d)"), turn_ps[0][:, 0:NC * DK])\
                 .then_inc(v_ready, 1)
                for t in range(NC):
                    row_max(b, t)
                    if t >= 1:
                        copy_turned_low(b, t - 1)
                    if t == TILES + 1:
                        scale_rows(b, 0)
                    if t > TILES + 1:
                        if isinstance(b, int) and b == 0:
                            dve.wait_ge(drive_loaded, 16 * DRIVE_LOADS)
                        add_output(b, t - TILES - 2)
                if more:
                    scale_k(b + 1)
                copy_turned_low(b, NC - 1)
                for t in range(2, TILES):
                    add_output(b, t)
                scale_rows(b, 1)
                for t in range(TILES, NC):
                    add_output(b, t)

            for c in range(NC):
                dve.wait_ge(coup_loaded[c], 16)
                last = V.tensor_reduce(col_max[:, c:c + 1], coup_stage(c), AX.X, ALU.max,
                                       apply_absolute_value=True)
            last.then_inc(maxes_ready, 1)
            dve.wait_ge(maxes_ready, 1)
            V.tensor_reduce(all_max[:, :], col_max[:, :], AX.X, ALU.max).then_inc(maxes_ready, 1)
            scale_k(0)
            dve.wait_ge(max_turned, 1)
            V.tensor_reduce(top[:, :], small_ps[0:1, 0:P], AX.X, ALU.max).then_inc(top_ready, 1)
            dve.wait_ge(max_spread, 1)
            V.tensor_scalar(all_max[:, :], small_ps[:, 0:1], 2.0 ** -100, 2.0 ** 100, ALU.max, ALU.min)\
             .then_inc(setup, 1)
            dve.wait_ge(setup, 1)
            V.tensor_scalar(power[:, :].bitcast(I32), all_max[:, :].bitcast(I32), 0x7f800000, None,
                            ALU.bitwise_and).then_inc(setup, 1)
            dve.wait_ge(setup, 2)
            V.reciprocal(inv_power[:, :], power[:, :]).then_inc(setup, 1)
            dve.wait_ge(setup, 3)
            V.tensor_scalar(coup_scale[:, :], inv_power[:, :], 2.0 ** COUP_EXP, None, ALU.mult)\
             .then_inc(scale_ready, 1)
            for s in range(STAGES):
                last = V.tensor_scalar(step_scale[:, s:s + 1], power[:, :], 2.0 ** -COUP_EXP,
                                       STEP[s] / TANH_SCALE, ALU.mult, ALU.mult)
            last.then_inc(setup, 1)
            dve.wait_ge(scale_ready, 1)
            for c in range(NC):
                dve.wait_ge(coup_high, c + 1)
                V.scalar_tensor_tensor(out=coup[:, c, 1, :], in0=coup_stage(c), scalar=coup_scale[:, 0:1],
                                       in1=coup[:, c, 0, :], op0=ALU.mult, op1=ALU.subtract)\
                 .then_inc(coup_low, 1)
            attend(0, True)
            with dve.Fori(1, B - 1) as b:
                attend(b, True)
            attend(B - 1, False)

            V.memset(tanh_parts[:, :, :, :], 0.0)
            V.tensor_copy(q_st[0][:, :], cond_sb[:, :, :].rearrange("p c b -> p (c b)"))
            V.tensor_scalar(p_st[:, :], cond_sb[:, :, :].rearrange("p c b -> p (c b)"), -SHIFT, None, ALU.add)
            V.memset(z[:, :], 0.0).then_inc(setup, 1)
            dve.wait_ge(setup, 5)
            for c in range(NC):
                last = V.tensor_scalar(cols(bias_b, (c, c + 1)), cols(z, (c, c + 1)), bias_sb[:, c:c + 1],
                                       -SHIFT, ALU.add, ALU.add)
            last.then_inc(setup, 1)
            dve.wait_ge(setup, 6)
            for j in range(NCH):
                V.engine_nop().then_inc(q_next[j], 1)
            V.tensor_tensor(drive_b[:, :], steps[:, 0, :], bias_b[:, :], ALU.add).then_inc(setup, 1)
            dve.wait_ge(setup, 7)
            V.tensor_tensor(drive_p[:, :], drive_b[:, :], p_st[:, :], ALU.subtract)\
             .then_inc(drive_p_ready, 1)


            def add_high(s, j, now):
                if j == 0:
                    dve.wait_ge(base_ready, now)
                dve.wait_ge(product_done[j], now)
                axpy(by_block(half_sum, CHUNKS[j]), product(s, j, 0), step_scale[:, s:s + 1],
                     by_block(base, CHUNKS[j])).then_inc(half_ready[j], 1)

            def add_low(s, j, now):
                dve.wait_ge(half_ready[j], now)
                out = q_st[s + 1] if s + 1 < STAGES else q_raw
                axpy(by_block(out, CHUNKS[j]), product(s, j, 1), step_scale[:, s:s + 1],
                     by_block(half_sum, CHUNKS[j])).then_inc(q_next[j], 1)

            def split_low(parity, j, made):
                dve.wait_ge(high_ready[j], made)
                axpy(tanh_part(parity, j, 1), by_block(tanh_sb, CHUNKS[j]), TANH_SCALE,
                     tanh_part(parity, j, 0), ALU.subtract).then_inc(parts_ready[j], 1)

            def cubic_of(stage, count):
                dve.wait_ge(square_ready if stage else square0_ready, count)
                V.scalar_tensor_tensor(out=cubic[:, :], in0=(square if stage else square0)[:, :], scalar=-3.0,
                                       in1=q_st[stage][:, :], op0=ALU.add, op1=ALU.mult)\
                 .then_inc(cubic_ready, 1)

            def base_of(stage, made):
                dve.wait_ge(cubic_ready, made)
                axpy(base[:, :], cubic[:, :], -STEP[stage] / 3, [z, z2, z3, z][stage][:, :])\
                    .then_inc(base_ready, 1)

            def z_of_first():
                axpy(z[:, :], drive_p[:, :], DT / 2, q_st[0][:, :])

            def z_of_second():
                axpy(z2[:, :], g0[:, :], -DT / 2 * RISE, z[:, :])

            def y_of():
                axpy(y[:, :], drive_p[:, :], DT, q_st[0][:, :])

            def y_less_g0():
                axpy(y_less[:, :], g0[:, :], -DT * RISE * G1[0], y[:, :])

            def z_of_third():
                axpy(z3[:, :], rise[0][:, :], -DT * RISE * G1[1], y_less[:, :])

            def rise_of(stage):
                V.tensor_tensor(rise[stage - 1][:, :], q_st[stage][:, :], q_st[0][:, :], ALU.subtract)

            def q_sum_g0():
                axpy(q_sum[0][:, :], g0[:, :], Q_SUM[0] / (DT / 2), drive_p[:, :])

            def q_sum_r1():
                axpy(q_sum[1][:, :], q_sum[0][:, :], DT / 2 / Q_SUM[1], rise[0][:, :])

            def q_sum_r2():
                axpy(q_sum[2][:, :], rise[1][:, :], Q_SUM[2] / Q_SUM[1], q_sum[1][:, :])

            def z_without_last(now):
                dve.wait_ge(q_share_ready, now)
                axpy(z_rest[:, :], q_sum[2][:, :], THIRD * Q_SUM[1], q_share[:, :])

            def z_of_last(made):
                dve.wait_ge(q_next[NCH - 1], made)
                axpy(z[:, :], q_st[3][:, :], THIRD, z_rest[:, :])

            def g0_of():
                axpy(g0[:, :], p_st[:, :], -BETA, q_st[0][:, :])

            def p_sum_g0():
                axpy(p_sum[0][:, :], g0[:, :], P_SUM[0], q_st[0][:, :], ALU.subtract)

            def p_sum_r(k):
                axpy(p_sum[k][:, :], rise[k - 1][:, :], P_SUM[k], p_sum[k - 1][:, :])

            def p_sum_q3():
                V.tensor_tensor(p_sum[3][:, :], p_sum[2][:, :], q_st[3][:, :], ALU.add)

            def p_next():
                axpy(p_raw[:, :], p_sum[3][:, :], DT / 6 * EPS, p_st[:, :])

            def clip_p():
                V.tensor_scalar(p_st[:, :], p_raw[:, :], -CLAMP - SHIFT, CLAMP - SHIFT, ALU.max, ALU.min)\
                 .then_inc(p_ready, STAGES)

            def look_ahead(at):
                V.tensor_tensor(drive_b[:, :], drive_cols[:, bass.ds(at, COLS)], bias_b[:, :], ALU.add)

            def drive_less_p(now):
                dve.wait_ge(p_ready, now)
                V.tensor_tensor(drive_p[:, :], drive_b[:, :], p_st[:, :], ALU.subtract)

            def clip_q(made):
                dve.wait_ge(q_next[NCH - 1], made)
                V.tensor_scalar(q_st[0][:, :], q_raw[:, :], -CLAMP, CLAMP, ALU.max, ALU.min)\
                 .then_inc(clipped, 1)

            def square_of_clipped(steps_done):
                dve.wait_ge(clipped, steps_done)
                V.tensor_tensor(square0[:, :], q_st[0][:, :], q_st[0][:, :], ALU.mult)\
                 .then_inc(square0_ready, 1)

            def trace(at):
                at = drive_cols[:, bass.ds(at, COLS)]
                V.tensor_tensor(at, at, q_st[0][:, :], ALU.add).then_inc(traced, 1)

            dve.wait_ge(drive_p_ready, 1)
            z_of_first()
            V.tensor_tensor(square0[:, :], q_st[0][:, :], q_st[0][:, :], ALU.mult).then_inc(setup, 1)
            for j in range(NCH):
                split_low(0, j, 1)
            dve.wait_ge(setup, 8)
            V.scalar_tensor_tensor(out=cubic[:, :], in0=square0[:, :], scalar=-3.0, in1=q_st[0][:, :],
                                   op0=ALU.add, op1=ALU.mult).then_inc(cubic_ready, 1)
            base_of(0, 1)

            def stage(s, now):
                parity = (s + 1) % 2
                if s == 2:
                    rise_of(2)
                if s == 3:
                    p_sum_q3()
                add_high(s, 0, now)
                add_high(s, 1, now)
                add_low(s, 0, now)
                add_low(s, 1, now)
                if s == 0:
                    g0_of()
                    y_of()
                if s == 1:
                    rise_of(1)
                    p_sum_g0()
                if s == 2:
                    q_sum_r2()
                    p_sum_r(2)
                if s == 3:
                    p_next()
                    look_ahead((now + STAGES) * (COLS // STAGES))
                made = after(now)
                add_high(s, 2, now)
                split_low(parity, 0, made)
                split_low(parity, 1, made)
                add_low(s, 2, now)
                add_high(s, 3, now)
                if s == 0:
                    z_of_second()
                if s == 1:
                    z_of_third()
                if s == 2:
                    z_without_last(now)
                if s == 3:
                    clip_p()
                    steps_done = steps_until(now)
                add_low(s, 3, now)
                if s == 0:
                    y_less_g0()
                if s == 1:
                    q_sum_r1()
                if s == 2:
                    trace((now - 3) * (COLS // STAGES))
                if s == 3:
                    drive_less_p(now)
                    clip_q(made)
                split_low(parity, 2, made)
                if s == 0:
                    q_sum_g0()
                if s == 1:
                    p_sum_r(1)
                if s == 2:
                    z_of_last(made)
                if s == 3:
                    square_of_clipped(steps_done)
                    z_of_first()
                    split_low(parity, 3, made)
                    cubic_of(0, steps_done)
                else:
                    cubic_of(s + 1, made)
                    split_low(parity, 3, made)
                base_of((s + 1) % STAGES, made)
                return made

            def after(now):
                return now + 1 if isinstance(now, int) else dve.snap(now + 1)

            def steps_until(now):
                return now // STAGES if isinstance(now, int) else dve.snap(now >> 2)

            order = [(s + 1) % STAGES for s in range(STAGES)] * UNROLLED
            stage(0, 1)
            with dve.Fori(2, 2 + STAGES * (STEPS - UNROLLED), STAGES * UNROLLED) as now:
                for s in order:
                    now = stage(s, now)
            now = 2 + STAGES * (STEPS - UNROLLED)
            for s in order[:-1]:
                now = stage(s, now)
            trace(STEPS * COLS)


def kernel(x, cond_2048, L0_cond_Wq, L0_cond_Wk, L0_cond_Wv, L0_cond_Wo, L1_cond_coupling, L1_cond_bias):
    import numpy as np
    import concourse.bacc as bacc
    from concourse.bass_utils import run_bass_kernel_spmd

    x, cond, coupling, bias = (np.asarray(a) for a in (x, cond_2048, L1_cond_coupling, L1_cond_bias))
    arrays = {
        "x": x,
        "x_pt": x.reshape(B, T, NC, P).transpose(3, 1, 2, 0).reshape(P, T, COLS),
        "cond": cond,
        "cond_p": cond.reshape(B, NC, P).transpose(2, 1, 0),
        "wq": np.asarray(L0_cond_Wq)[1],
        "wk": np.asarray(L0_cond_Wk)[1],
        "wv": np.asarray(L0_cond_Wv)[1],
        "wo": np.asarray(L0_cond_Wo),
        "coupling_t": coupling.T,
        "bias_p": bias.reshape(NC, P).T,
    }
    arrays = {k: np.ascontiguousarray(a) for k, a in arrays.items()}
    nc = bacc.Bacc("TRN2", target_bir_lowering=False, num_devices=1,
                   dynamic_dma_scratch_size=1024)
    args = [nc.dram_tensor(f"in_{k}", a.shape, mybir.dt.from_np(a.dtype), kind="ExternalInput").ap()
            for k, a in arrays.items()]
    out = nc.dram_tensor("out_pt", (P, T, COLS), F32, kind="ExternalOutput").ap()
    build(nc, *args, out)
    r = run_bass_kernel_spmd(nc, [{f"in_{k}": a for k, a in arrays.items()}], core_ids=[0])
    got = np.asarray(r.results[0]["out_pt"])
    return np.ascontiguousarray(got.reshape(P, T, NC, B).transpose(3, 1, 2, 0).reshape(B, T, N))
```
